# Optimizing a Trainium2 kernel written in Bass

```python
import numpy as np
import jax
import jax.numpy as jnp

def _softmax(x, axis=-1):
    return jax.nn.softmax(x, axis=axis)

def _gelu(x):
    return jax.nn.gelu(x, approximate=True)

def _silu(x):
    return jax.nn.silu(x)

def _sigmoid(x):
    return jax.nn.sigmoid(x)

def _layernorm(x, axis=-1, eps=1e-05):
    m = jnp.mean(x, axis=axis, keepdims=True)
    v = jnp.var(x, axis=axis, keepdims=True)
    return (x - m) / jnp.sqrt(v + eps)

def _scatter_add(tgt, idx, src, axis=0):
    return tgt.at[idx].add(src)

def _segment_sum(src, seg, n):
    return jax.ops.segment_sum(src, seg, n)
kernel_name = 'mk_seq_postln_d1_jaxref_r8_c61703'

def setup_inputs(seed: int=0):
    np.random.seed(seed)
    _w = jnp.asarray

    def _L0_attn_setup():
        import jax, jax.numpy as jnp
        import numpy as np
        D_MODEL = 256
        N_HEADS = 16
        HEAD_DIM = D_MODEL // N_HEADS
        ROPE_THETA = 10000.0
        BATCH = 2
        SEQ_LEN = 256

        def _apply_rope(x):
            S = x.shape[2]
            inv_freq = 1.0 / ROPE_THETA ** (jnp.arange(0, HEAD_DIM, 2, dtype=jnp.float32) / HEAD_DIM)
            t = jnp.arange(S, dtype=jnp.float32)
            freqs = jnp.outer(t, inv_freq)
            cos = jnp.cos(freqs)
            sin = jnp.sin(freqs)
            x1 = x[..., 0::2]
            x2 = x[..., 1::2]
            rot = jnp.stack([x1 * cos - x2 * sin, x1 * sin + x2 * cos], axis=-1)
            return rot.reshape(x.shape)
        key = jax.random.key(seed)
        ks = jax.random.split(key, 5)
        scale = 1.0 / np.sqrt(D_MODEL)
        x = jax.random.normal(ks[0], (BATCH, SEQ_LEN, D_MODEL), dtype=jnp.float32)
        Wq = jax.random.normal(ks[1], (D_MODEL, D_MODEL), dtype=jnp.float32) * scale
        Wk = jax.random.normal(ks[2], (D_MODEL, D_MODEL), dtype=jnp.float32) * scale
        Wv = jax.random.normal(ks[3], (D_MODEL, D_MODEL), dtype=jnp.float32) * scale
        Wo = jax.random.normal(ks[4], (D_MODEL, D_MODEL), dtype=jnp.float32) * scale
        return {'x': x, 'Wq': Wq, 'Wk': Wk, 'Wv': Wv, 'Wo': Wo}
    _L0_attn_in = _L0_attn_setup()

    def _L0_ffn_setup():
        import jax, jax.numpy as jnp
        import numpy as np

        def _sparsify_2to4(h):
            B, S, I = h.shape
            g = h.reshape(B, S, I // 4, 4)
            a = jnp.abs(g)
            _, idx = jax.lax.top_k(a, 2)
            pos = jnp.arange(4)
            mask = (pos == idx[..., 0:1]) | (pos == idx[..., 1:2])
            return (g * mask.astype(g.dtype)).reshape(B, S, I)
        key = jax.random.key(seed)
        k1, k2, k3, k4 = jax.random.split(key, 4)
        B, S, H, I = (4, 256, 256, 1024)
        x = jax.random.normal(k1, (B, S, H), dtype=jnp.float32)
        w_gate = jax.random.normal(k2, (H, I), dtype=jnp.float32) / np.sqrt(H)
        w_up = jax.random.normal(k3, (H, I), dtype=jnp.float32) / np.sqrt(H)
        w_down = jax.random.normal(k4, (I, H), dtype=jnp.float32) / np.sqrt(I)
        return {'x': x, 'w_gate': w_gate, 'w_up': w_up, 'w_down': w_down}
    _L0_ffn_in = _L0_ffn_setup()
    _d = {'L0_attn_x': _L0_attn_in['x'], 'L0_attn_Wq': _L0_attn_in['Wq'], 'L0_attn_Wk': _L0_attn_in['Wk'], 'L0_attn_Wv': _L0_attn_in['Wv'], 'L0_attn_Wo': _L0_attn_in['Wo'], 'L0_ffn_w_gate': _L0_ffn_in['w_gate'], 'L0_ffn_w_up': _L0_ffn_in['w_up'], 'L0_ffn_w_down': _L0_ffn_in['w_down']}
    _x0 = _d['L0_attn_x']
    _d['L0_attn_x'] = jax.random.normal(jax.random.fold_in(jax.random.key(seed), 1), (8, 512, 256), dtype=_x0.dtype)
    del _x0
    return _d

def reference(L0_attn_x, L0_attn_Wq, L0_attn_Wk, L0_attn_Wv, L0_attn_Wo, L0_ffn_w_gate, L0_ffn_w_up, L0_ffn_w_down):

    def _L0_attn_ref(x, Wq, Wk, Wv, Wo):
        import jax, jax.numpy as jnp
        import numpy as np
        D_MODEL = 256
        N_HEADS = 16
        HEAD_DIM = D_MODEL // N_HEADS
        ROPE_THETA = 10000.0
        BATCH = 2
        SEQ_LEN = 256

        def _apply_rope(x):
            S = x.shape[2]
            inv_freq = 1.0 / ROPE_THETA ** (jnp.arange(0, HEAD_DIM, 2, dtype=jnp.float32) / HEAD_DIM)
            t = jnp.arange(S, dtype=jnp.float32)
            freqs = jnp.outer(t, inv_freq)
            cos = jnp.cos(freqs)
            sin = jnp.sin(freqs)
            x1 = x[..., 0::2]
            x2 = x[..., 1::2]
            rot = jnp.stack([x1 * cos - x2 * sin, x1 * sin + x2 * cos], axis=-1)
            return rot.reshape(x.shape)
        B, S, _ = x.shape
        q = (x @ Wq.T).reshape(B, S, N_HEADS, HEAD_DIM).transpose(0, 2, 1, 3)
        k = (x @ Wk.T).reshape(B, S, N_HEADS, HEAD_DIM).transpose(0, 2, 1, 3)
        v = (x @ Wv.T).reshape(B, S, N_HEADS, HEAD_DIM).transpose(0, 2, 1, 3)
        q = _apply_rope(q)
        k = _apply_rope(k)
        scores = jnp.einsum('bhqd,bhkd->bhqk', q, k) / np.sqrt(HEAD_DIM).astype(np.float32)
        causal = jnp.tril(jnp.ones((S, S), dtype=bool))
        scores = jnp.where(causal, scores, -jnp.inf)
        attn = jax.nn.softmax(scores, axis=-1)
        out = jnp.einsum('bhqk,bhkd->bhqd', attn, v)
        out = out.transpose(0, 2, 1, 3).reshape(B, S, N_HEADS * HEAD_DIM)
        return out @ Wo.T

    def _L0_ffn_ref(x, w_gate, w_up, w_down):
        import jax, jax.numpy as jnp
        import numpy as np

        def _sparsify_2to4(h):
            B, S, I = h.shape
            g = h.reshape(B, S, I // 4, 4)
            a = jnp.abs(g)
            _, idx = jax.lax.top_k(a, 2)
            pos = jnp.arange(4)
            mask = (pos == idx[..., 0:1]) | (pos == idx[..., 1:2])
            return (g * mask.astype(g.dtype)).reshape(B, S, I)
        h = jax.nn.silu(jnp.einsum('bsh,hi->bsi', x, w_gate)) * jnp.einsum('bsh,hi->bsi', x, w_up)
        h_sparse = _sparsify_2to4(h)
        return jnp.einsum('bsi,ih->bsh', h_sparse, w_down)
    x = L0_attn_x
    x = _layernorm(x + _L0_attn_ref(x, L0_attn_Wq, L0_attn_Wk, L0_attn_Wv, L0_attn_Wo), axis=-1)
    x = _layernorm(x + _L0_ffn_ref(x, L0_ffn_w_gate, L0_ffn_w_up, L0_ffn_w_down), axis=-1)
    return x

_drawn_inputs = setup_inputs


def setup_inputs(seed=0):
    import zlib

    import numpy as np

    out = dict(_drawn_inputs(seed))
    spreads = {}
    factors = {}
    for name, (base, spread) in spreads.items():
        noise = np.random.default_rng([zlib.crc32(name.encode()), seed]).standard_normal(out[name].shape)
        drawn = base * np.exp(spread * noise) if base else spread * noise
        out[name] = jnp.asarray(drawn.astype(out[name].dtype))
    for name, factor in factors.items():
        out[name] = (out[name] * factor).astype(out[name].dtype)
    return out
```

```python
from contextlib import ExitStack

import concourse.bass as bass
from concourse import mybir

f32 = mybir.dt.float32
f32r = mybir.dt.float32r
bf16 = mybir.dt.bfloat16
ALU = mybir.AluOpType
ACT = mybir.ActivationFunctionType
AX = mybir.AxisListType

P = 128
B, S, D = 8, 512, 256
H, DH = 16, 16
I = 1024
NT = S // P
NC = D // P
HH = H // 2
EPS = 1e-5
NEG = -1e30
G4 = 4
NG = H // G4

ROWS_QK = 3 * DH
ROWS_ALL = ROWS_QK + 2

WTILE = [0, 2, 1, 3]
WIN = 5
DIAG, OFF13, OFF2 = range(3)

STEPS = H // 2 * NT
T_AT = {n: n for n in range(4)}
V_AT = {5 + 3 * t: t for t in range(NT)}
QK_AT = {7 + 3 * t: t for t in range(NT)}
PV_AT = {8 * (j + 1) + 3: j for j in range(NG - 1)}
FILLS = 6 * HH
FILL_FROM = 8
FILL_E = STEPS - FILL_FROM
FILL_W = 2
FILL_LAST = FILLS - FILL_E - 8 * FILL_W
ROPE_FROM = 4


def wait_apart(engine, spare, semaphore, value):
    engine.wait_ge(semaphore, value)
    if not isinstance(value, int):
        engine.sem_inc(spare, 1)


def attention_phase(nc, x, xT, wqkvT, woT, cos, sin, parts, maxima, x1):
    ctx = ExitStack()
    with ctx:
        def sb(name, shape, dt=f32):
            return ctx.enter_context(nc.sbuf_tensor(name, shape, dt))

        def sem(name):
            return ctx.enter_context(nc.semaphore(name))

        wqkv_h = sb("wqkv_h", [P, NC, 3 * D], f32r)
        wqkv_l = sb("wqkv_l", [P, NC, 3 * D], f32r)
        wo_h = sb("wo_h", [P, NC, D], f32r)
        wo_l = sb("wo_l", [P, NC, D], f32r)
        cos_sb = sb("cos_sb", [P, NT, 2, DH])
        sin_sb = sb("sin_sb", [P, NT, 2, DH])
        ident = sb("ident", [P, P])
        ident_b = sb("ident_b", [P, P], bf16)
        mask_b = sb("mask_b", [P, NT, P], bf16)
        mhalf = sb("mhalf", [P, NT])
        xT_sb = sb("xT_sb", [P, NC, S])
        xh = [sb(f"xh{i}", [P, NC, S], f32r) for i in range(2)]
        xl = [sb(f"xl{i}", [P, NC, S], f32r) for i in range(2)]
        qk_raw = sb("qk_raw", [P, 2, 2 * D])
        rope_s = sb("rope_s", [P, 2 * D])
        qk_rot = sb("qk_rot", [P, NT, 2 * D])
        part_h = sb("part_h", [P, 2, S], f32r)
        part_l = sb("part_l", [P, 2, S], f32r)
        q_st = [sb(f"q_st{i}", [P, HH, S], f32r) for i in range(2)]
        k_st = [sb(f"k_st{i}", [P, HH, S], f32r) for i in range(2)]
        v_sb = [sb(f"v_sb{i}", [P, NT, H, 32]) for i in range(2)]
        bmax = sb("bmax", [P, H, NT * WIN])
        nmax = sb("nmax", [P, H, NT])
        nmax_h = sb("nmax_h", [P, H, NT], f32r)
        nmax2 = sb("nmax2", [P, NT, 2 * H])
        nmaxT = sb("nmaxT", [2 * H, S], f32r)
        prob = [[sb(f"prob{kt}_{i}", [P, G4, S - P * kt]) for i in range(2 if kt < 2 else 1)]
                for kt in range(NT)]
        oT_sb = sb("oT_sb", [P, NG, S])
        rden = sb("rden", [P, H, 1])
        attn = sb("attn", [P, NT, D])
        aT_h = sb("aT_h", [P, NC, S], f32r)
        aT_l = sb("aT_l", [P, NC, S], f32r)
        y_sb = sb("y_sb", [P, NT, D])
        stats = sb("stats", [P, NT, 6])
        meanvar = sb("meanvar", [P, NT, 2])
        vare = sb("vare", [P, NT])
        rstd = sb("rstd", [P, NT])

        mx_ps = [ctx.enter_context(nc.psum_tensor(f"mx_ps{i}", [P, S], f32)) for i in range(2)]
        ex_ps = [ctx.enter_context(nc.psum_tensor(f"ex_ps{i}", [P, 2, S], f32)) for i in range(2)]
        pv_ps = ctx.enter_context(nc.psum_tensor("pv_ps", [P, S], f32))
        mi_ps = ctx.enter_context(nc.psum_tensor("mi_ps", [P, S], f32))

        w_in = sem("w_in")
        w_split = sem("w_split")
        const_s = sem("const_s")
        idb_s = sem("idb_s")
        set_s = sem("set_s")
        xT_in = sem("xT_in")
        x_in = sem("x_in")
        x_split = sem("x_split")
        qk_done = sem("qk_done")
        qk_ev = sem("qk_ev")
        v_done = sem("v_done")
        v_ev = sem("v_ev")
        rope = sem("rope")
        qkT_done = sem("qkT_done")
        qkT_h = sem("qkT_h")
        qkT_l = sem("qkT_l")
        spill = [sem(f"spill{i}") for i in range(2)]
        stack = sem("stack")
        mx_done = sem("mx_done")
        mx_read = sem("mx_read")
        nm = sem("nm")
        nmT_done = sem("nmT_done")
        nmT_ev = sem("nmT_ev")
        nm_spill = sem("nm_spill")
        nm_dma = sem("nm_dma")
        ex_done = sem("ex_done")
        ex_act = sem("ex_act")
        masked = sem("masked")
        pv_done = sem("pv_done")
        oT_ev = sem("oT_ev")
        o_done = sem("o_done")
        rden_s = sem("rden_s")
        attn_s = sem("attn_s")
        aT_done = sem("aT_done")
        aT_hs = sem("aT_hs")
        aT_ls = sem("aT_ls")
        wo_done = sem("wo_done")
        res = sem("res")
        stat = sem("stat")
        mv = sem("mv")
        rs = sem("rs")
        ln = sem("ln")
        x1_out = sem("x1_out")
        spare_pool, spare_dve = sem("spare_pool"), sem("spare_dve")
        PER_T, PER_SPILL, PER_STACK, PER_NM = 4, 4 * 16, 8 * 16, 2 * 16

        block = ctx.enter_context(nc.Block())

        @block.sync
        def _(sp):
            sp.dma_start(xT_sb[:], xT[0].rearrange("(c p) n -> p c n", p=P)).then_inc(xT_in, 16)
            sp.dma_start(prob[0][0][:, 0:NC, :].rearrange("p a b -> p (a b)")[:, 0:2 * S],
                         wqkvT.rearrange("(c p) n -> p c n", p=P)[:, :, 0:S]).then_inc(w_in, 16)
            sp.dma_start(prob[0][1][:, 0, :].rearrange("p (c n) -> p c n", c=NC),
                         wqkvT.rearrange("(c p) n -> p c n", p=P)[:, :, S:]).then_inc(w_in, 16)
            sp.dma_start(prob[0][1][:, 1, :].rearrange("p (c n) -> p c n", c=NC),
                         woT.rearrange("(c p) n -> p c n", p=P)).then_inc(w_in, 16)
            for dst, src in ((cos_sb, cos), (sin_sb, sin)):
                sp.dma_start(dst[:], src.rearrange("(t p) a d -> p t a d", p=P)).then_inc(w_in, 16)

            def load_xT(b):
                sp.wait_ge(x_split, 2 * b)
                sp.dma_start(xT_sb[:], xT[b].rearrange("(c p) n -> p c n", p=P)).then_inc(xT_in, 16)

            def spill_parts(b, n, par):
                dst = parts[par, n // 2, 8 * (n % 2):8 * (n % 2) + 8]
                for e, (src, there) in enumerate(((part_h, qkT_h), (part_l, qkT_l))):
                    sp.wait_ge(there, PER_T * b + n + 1)
                    sp.dma_start(dst[:, e], src[:, n % 2, :].bitcast(f32)).then_inc(spill[n % 2], 16)

            def fill_stack(b, qk, par):
                for i in range(2):
                    sp.wait_ge(spill[i], PER_SPILL * b + 32 * (qk + 1))
                dst = (q_st, k_st)[qk][par]
                for hp in range(2):
                    src = parts[par, qk].rearrange("(hh hp) e d n -> hp (e d) hh n", hp=2)[hp]
                    for at, n in (((0, 2), (2, 1)), ((0, 1), (1, 2)))[qk]:
                        lo = 64 * hp + DH * at
                        sp.dma_start(dst[lo:lo + DH * n].bitcast(f32), src[0:DH * n]).then_inc(stack, 16)

            def place_maxima(b, par):
                sp.wait_ge(nmT_ev, b + 1)
                sp.dma_start(maxima, nmaxT[:].bitcast(f32)).then_inc(nm_spill, 16)
                sp.wait_ge(nm_spill, 16 * (b + 1))
                for hp in range(2):
                    at = 64 * hp + ROWS_QK
                    sp.dma_start(q_st[par][at:at + 2].bitcast(f32),
                                 maxima.rearrange("(hp hh e) n -> hp e hh n", hp=2, e=2)[hp]
                                 ).then_inc(nm_dma, 16)

            def load_x(b):
                sp.dma_start(y_sb[:], x[b].rearrange("(t p) d -> p t d", p=P)).then_inc(x_in, 16)

            def store_x1(b):
                sp.wait_ge(ln, NT * (b + 1))
                sp.dma_start(x1[b].rearrange("(t p) d -> p t d", p=P), y_sb[:]).then_inc(x1_out, 16)
                sp.wait_ge(x1_out, 16 * (b + 1))

            def iteration(b, par, E=True, M=True, F=True):
                if F:
                    load_xT(b + 2)
                if M:
                    for n in range(4):
                        spill_parts(b + 1, n, 1 - par)
                        if n % 2:
                            fill_stack(b + 1, n // 2, 1 - par)
                    place_maxima(b + 1, 1 - par)
                if E:
                    store_x1(b)
                if M:
                    load_x(b + 1)

            sp.wait_ge(set_s, 4)
            iteration(-1, 1, E=False)
            with sp.Fori(0, 3) as i:
                iteration(2 * i, 0)
                iteration(2 * i + 1, 1)
            iteration(6, 0, F=False)
            iteration(7, 1, M=False, F=False)

        @block.gpsimd
        def _(pool):
            nc.gpsimd.memset(ident[:], 0.0).then_inc(const_s, 1)
            nc.gpsimd.memset(mask_b[:], 0.0).then_inc(const_s, 1)
            nc.gpsimd.memset(mhalf[:], -0.5).then_inc(const_s, 1)
            pool.wait_ge(const_s, 3)
            nc.gpsimd.affine_select(out=ident[:], in_=ident[:], compare_op=ALU.not_equal, fill=1.0, base=0,
                                    pattern=[[-1, P]], channel_multiplier=1).then_inc(const_s, 1)
            nc.gpsimd.affine_select(out=mask_b[:], in_=mask_b[:], compare_op=ALU.is_ge, fill=NEG, base=0,
                                    pattern=[[0, NT], [-1, P]], channel_multiplier=1).then_inc(const_s, 1)
            pool.wait_ge(const_s, 5)
            nc.gpsimd.tensor_copy(ident_b[:], ident[:]).then_inc(idb_s, 1)

            def split_x(b, par, first=False):
                if not first:
                    pool.wait_ge(v_done, NT * (b - 1))
                wait_apart(pool, spare_pool, xT_in, 16 * (b + 1))
                nc.gpsimd.tensor_scalar(xh[par][:], xT_sb[:], 1.0, None, ALU.mult).then_inc(x_split, 1)
                pool.wait_ge(x_split, 2 * b + 1)
                nc.gpsimd.tensor_tensor(xl[par][:], xT_sb[:], xh[par][:].bitcast(f32),
                                        ALU.subtract).then_inc(x_split, 1)

            def rope_op(b, n, first=False):
                t, k = n // 3, n % 3
                raw = qk_raw[:, t % 2, :].rearrange("p (a h d) -> p a h d", a=2, h=H)
                rot = qk_rot[:, t, :]
                if k == 0:
                    pool.wait_ge(qk_ev, NT * b + t + 1)
                    if not first:
                        pool.wait_ge(qkT_done, PER_T * b)
                    nc.gpsimd.tensor_tensor(rot.rearrange("p (a h d) -> p a h d", a=2, h=H), raw,
                                            cos_sb[:, t, :, None, :].broadcast_to([P, 2, H, DH]),
                                            ALU.mult).then_inc(rope, 1)
                elif k == 1:
                    if not (first and t == 0 and b == 0):
                        pool.wait_ge(rope, 3 * NT * b + n - 1)
                    nc.gpsimd.tensor_tensor(rope_s[:].rearrange("p (a h d) -> p a h d", a=2, h=H), raw,
                                            sin_sb[:, t, :, None, :].broadcast_to([P, 2, H, DH]),
                                            ALU.mult).then_inc(rope, 1)
                else:
                    pool.wait_ge(rope, 3 * NT * b + n)
                    nc.gpsimd.tensor_tensor(rot.rearrange("p (n e) -> p n e", e=2),
                                            rot.rearrange("p (n e) -> p n e", e=2),
                                            rope_s[:].rearrange("p (n e) -> p n e", e=2)[:, :, ::-1],
                                            ALU.add).then_inc(rope, 1)

            def mask(b, m):
                j, kt = m // NT, m % NT
                p = prob[kt][j % 2 if kt < 2 else 0]
                wait_apart(pool, spare_pool, ex_act, STEPS * b + 2 * m + 2)
                nc.gpsimd.affine_select(out=p[:, :, 0:P], in_=p[:, :, 0:P], compare_op=ALU.is_ge, fill=0.0,
                                        base=0, pattern=[[0, G4], [1, P]],
                                        channel_multiplier=-1).then_inc(masked, 1)

            def iteration(b, par, E=True, M=True, F=True, first=False):
                if F:
                    split_x(b + 2, par, first)
                for m in range(4 * NG):
                    if E:
                        mask(b, m)
                    if F and ROPE_FROM <= m < ROPE_FROM + 3 * NT // 2:
                        rope_op(b + 2, 2 * (m - ROPE_FROM))
                        rope_op(b + 2, 2 * (m - ROPE_FROM) + 1)
                if E:
                    wait_apart(pool, spare_pool, mv, NT * (b + 1))
                    nc.gpsimd.tensor_scalar(vare[:], meanvar[:, :, 1], EPS, None, ALU.add).then_inc(rs, 1)
                    pool.wait_ge(rs, 2 * b + 1)
                    nc.gpsimd.tensor_tensor(rstd[:], vare[:], mhalf[:], ALU.pow).then_inc(rs, 1)

            split_x(0, 0, first=True)
            pool.wait_ge(w_in, 5 * 16)
            for n in range(3 * NT):
                rope_op(0, n, first=True)
            iteration(-1, 1, E=False, first=True)
            with pool.Fori(0, 3) as i:
                iteration(2 * i, 0)
                iteration(2 * i + 1, 1)
            iteration(6, 0, F=False)
            iteration(7, 1, M=False, F=False)

        @block.scalar
        def _(act):
            act.wait_ge(w_in, 5 * 16)
            raw_qk = prob[0][0][:, 0:NC, :]
            raw_v = prob[0][1][:, 0, :].rearrange("p (c n) -> p c n", c=NC)
            raw_o = prob[0][1][:, 1, :].rearrange("p (c n) -> p c n", c=NC)
            nc.scalar.activation(wqkv_h[:, :, 0:S], raw_qk, ACT.Copy).then_inc(w_split, 1)
            nc.scalar.activation(wqkv_h[:, :, S:], raw_v, ACT.Copy).then_inc(w_split, 1)
            nc.scalar.activation(wo_h[:], raw_o, ACT.Copy).then_inc(w_split, 1)

            def ev_qk(b, t):
                act.wait_ge(qk_done, NT * b + t + 1)
                if not (isinstance(b, int) and NT * b + t < 2):
                    act.wait_ge(rope, 3 * (NT * b + t - 1) - 1)
                nc.scalar.activation(qk_raw[:, t % 2, :], mi_ps[:], ACT.Copy).then_inc(qk_ev, 1)

            def ev_v(b, t, par):
                act.wait_ge(v_done, NT * b + t + 1)
                nc.scalar.activation(v_sb[par][:, t, :, 0:DH],
                                     mi_ps[:, 0:D].rearrange("p (h d) -> p h d", h=H),
                                     ACT.Copy).then_inc(v_ev, 1)

            def high_qkT(b, n):
                act.wait_ge(qkT_done, PER_T * b + n + 1)
                if n >= 2:
                    act.wait_ge(spill[n % 2], PER_SPILL * b + 32)
                nc.scalar.activation(part_h[:, n % 2, :], mi_ps[:], ACT.Copy).then_inc(qkT_h, 1)

            def exp_step(b, s):
                j, kt, pr = s // 8, s % 8 // 2, s % 2
                p = prob[kt][j % 2 if kt < 2 else 0]
                act.wait_ge(ex_done, STEPS * b + s + 1)
                if kt < 2 and j >= 2:
                    act.wait_ge(pv_done, NG * b + j - 1)
                if kt >= 2 and j >= 1:
                    act.wait_ge(pv_done, NG * b + j)
                n = S - P * kt
                nc.scalar.activation(p[:, 2 * pr:2 * pr + 2, :], ex_ps[s % 2][:, :, 0:n],
                                     ACT.Exp).then_inc(ex_act, 1)

            def ev_oT(b, j):
                act.wait_ge(pv_done, NG * b + j + 1)
                nc.scalar.activation(oT_sb[:, j, :], pv_ps[:], ACT.Copy).then_inc(oT_ev, 1)

            def iteration(b, par, E=True, M=True, F=True):
                for s in range(STEPS):
                    if E:
                        exp_step(b, s)
                    if M and s in T_AT:
                        high_qkT(b + 1, T_AT[s])
                    if M and s in V_AT:
                        ev_v(b + 1, V_AT[s], 1 - par)
                    if F and s in QK_AT:
                        ev_qk(b + 2, QK_AT[s])
                    if E and s in PV_AT:
                        ev_oT(b, PV_AT[s])
                if E:
                    ev_oT(b, NG - 1)
                    for c in range(NC):
                        act.wait_ge(aT_done, NC * b + c + 1)
                        nc.scalar.activation(aT_h[:, c, :], mi_ps[:], ACT.Copy).then_inc(aT_hs, 1)
                if M:
                    act.wait_ge(nmT_done, b + 2)
                    if not (isinstance(b, int) and b < 0):
                        act.wait_ge(nm_spill, 16 * (b + 1))
                    nc.scalar.activation(nmaxT[:], mi_ps[0:2 * H, :], ACT.Copy).then_inc(nmT_ev, 1)

            act.wait_ge(set_s, 4)
            for t in range(NT):
                ev_qk(0, t)
            iteration(-1, 1, E=False)
            with act.Fori(0, 3) as i:
                iteration(2 * i, 0)
                iteration(2 * i + 1, 1)
            iteration(6, 0, F=False)
            iteration(7, 1, M=False, F=False)

        @block.vector
        def _(dve):
            for i in range(2):
                for lo in (32, 96):
                    nc.vector.memset(k_st[i][lo:lo + 32, :, :].bitcast(f32), 1.0)
                nc.vector.memset(v_sb[i][:], 1.0).then_inc(set_s, 1)
            nc.vector.memset(bmax[:], NEG).then_inc(set_s, 2)
            raw_qk = prob[0][0][:, 0:NC, :]
            raw_v = prob[0][1][:, 0, :].rearrange("p (c n) -> p c n", c=NC)
            raw_o = prob[0][1][:, 1, :].rearrange("p (c n) -> p c n", c=NC)
            dve.wait_ge(w_split, 3)
            nc.vector.tensor_tensor(wqkv_l[:, :, 0:S], raw_qk, wqkv_h[:, :, 0:S].bitcast(f32),
                                    ALU.subtract).then_inc(w_split, 1)
            nc.vector.tensor_tensor(wqkv_l[:, :, S:], raw_v, wqkv_h[:, :, S:].bitcast(f32),
                                    ALU.subtract).then_inc(w_split, 1)
            nc.vector.tensor_tensor(wo_l[:], raw_o, wo_h[:].bitcast(f32), ALU.subtract).then_inc(w_split, 1)

            def low_qkT(b, n):
                dve.wait_ge(qkT_h, PER_T * b + n + 1)
                nc.vector.tensor_tensor(part_l[:, n % 2, :], mi_ps[:], part_h[:, n % 2, :].bitcast(f32),
                                        ALU.subtract).then_inc(qkT_l, 1)

            def block_max(b, f):
                hh, kind, hp = f // 6, f % 6 // 2, f % 2
                h = 2 * hh + hp
                slots = bmax[:, h, :]
                dve.wait_ge(mx_done, FILLS * b + f + 1)
                out, n = {DIAG: (slots[:, 3:NT * WIN:WIN], NT), OFF13: (slots[:, 14:18], 4),
                          OFF2: (slots[:, 5:7], 2)}[kind]
                nc.vector.tensor_reduce(out=out, in_=mx_ps[hp][:, 0:n * P].rearrange("p (n k) -> p n k", n=n),
                                        axis=AX.X, op=ALU.max).then_inc(mx_read, 1)

            def negate_max(b):
                dve.wait_ge(mx_read, FILLS * (b + 1))
                nc.vector.tensor_reduce(out=nmax[:], in_=bmax[:].rearrange("p h (w s) -> p h w s", w=NT),
                                        axis=AX.X, op=ALU.max, negate=True).then_inc(nm, 1)
                dve.wait_ge(nm, 4 * b + 1)
                nc.vector.tensor_copy(nmax_h[:], nmax[:]).then_inc(nm, 1)
                dve.wait_ge(nm, 4 * b + 2)
                view = nmax2[:].rearrange("p w (hp hh e) -> p e hp hh w", hp=2, e=2)
                src = [a.rearrange("p (hh hp) w -> p hp hh w", hp=2) for a in (nmax[:], nmax_h[:].bitcast(f32))]
                nc.vector.tensor_copy(view[:, 0], src[1]).then_inc(nm, 1)
                nc.vector.tensor_tensor(view[:, 1], src[0], src[1], ALU.subtract).then_inc(nm, 1)

            def normalise(b, t):
                o = mi_ps[:].rearrange("p (h c) -> p h c", h=H)
                dve.wait_ge(o_done, NT * b + t + 1)
                nc.vector.reciprocal(rden[:], o[:, :, DH:DH + 1]).then_inc(rden_s, 1)
                dve.wait_ge(rden_s, NT * b + t + 1)
                nc.vector.tensor_tensor(attn[:, t, :].rearrange("p (h d) -> p h d", h=H), o[:, :, 0:DH],
                                        rden[:].broadcast_to([P, H, DH]), ALU.mult).then_inc(attn_s, 1)

            def low_aT(b, c):
                dve.wait_ge(aT_hs, NC * b + c + 1)
                nc.vector.tensor_tensor(aT_l[:, c, :], mi_ps[:], aT_h[:, c, :].bitcast(f32),
                                        ALU.subtract).then_inc(aT_ls, 1)

            def residual(b, u):
                dve.wait_ge(wo_done, 2 * b + u + 1)
                if u == 0:
                    dve.wait_ge(x_in, 16 * (b + 1))
                y = y_sb[:, 2 * u:2 * u + 2, :]
                nc.vector.tensor_tensor(y, mi_ps[:].rearrange("p (t d) -> p t d", t=2), y,
                                        ALU.add).then_inc(res, 1)

            def iteration(b, par, E=True, M=True, F=True):
                f = 0
                for s in range(STEPS):
                    if M and s in T_AT:
                        low_qkT(b + 1, T_AT[s])
                    if M and s >= FILL_FROM:
                        block_max(b + 1, s - FILL_FROM)
                f = FILL_E
                for k in range(8):
                    if E:
                        if k < 4:
                            normalise(b, k)
                        elif k < 6:
                            low_aT(b, k - 4)
                        else:
                            residual(b, k - 6)
                    if M:
                        for g in range(FILL_W):
                            block_max(b + 1, f + g)
                        f += FILL_W
                if E:
                    for t in range(NT):
                        dve.wait_ge(res, 2 * b + t // 2 + 1)
                        nc.vector.bn_stats(stats[:, t, :], y_sb[:, t, :]).then_inc(stat, 1)
                    for t in range(NT):
                        wait_apart(dve, spare_dve, stat, NT * b + t + 1)
                        nc.vector.bn_aggr(meanvar[:, t, :], stats[:, t, :]).then_inc(mv, 1)
                if M:
                    for g in range(FILL_LAST):
                        block_max(b + 1, f + g)
                    negate_max(b + 1)
                if E:
                    dve.wait_ge(rs, 2 * (b + 1))
                    for t in range(NT):
                        nc.vector.tensor_scalar(y_sb[:, t, :], y_sb[:, t, :], meanvar[:, t, 0:1],
                                                rstd[:, t:t + 1], ALU.subtract, ALU.mult).then_inc(ln, 1)

            iteration(-1, 1, E=False)
            with dve.Fori(0, 3) as i:
                iteration(2 * i, 0)
                iteration(2 * i + 1, 1)
            iteration(6, 0, F=False)
            iteration(7, 1, M=False, F=False)

        @block.tensor
        def _(pe):
            def product(out, lh, ll, rh, rl, chunks, inc):
                terms = [(a, r, c) for c in range(chunks) for a, r in ((lh, rh), (lh, rl), (ll, rh))]
                for n, (a, r, c) in enumerate(terms):
                    last = nc.tensor.matmul(out, a(c), r(c), start=n == 0, stop=n == len(terms) - 1)
                last.then_inc(inc, 1)

            def project_qk(b, t, par):
                tok = slice(P * t, P * t + P)
                product(mi_ps[:], lambda c: xh[par][:, c, tok], lambda c: xl[par][:, c, tok],
                        lambda c: wqkv_h[:, c, 0:2 * D], lambda c: wqkv_l[:, c, 0:2 * D], NC, qk_done)

            def project_v(b, t, par):
                tok = slice(P * t, P * t + P)
                product(mi_ps[:, 0:D], lambda c: xh[par][:, c, tok], lambda c: xl[par][:, c, tok],
                        lambda c: wqkv_h[:, c, 2 * D:], lambda c: wqkv_l[:, c, 2 * D:], NC, v_done)

            def transpose_qk(b, n):
                for t in range(NT):
                    last = nc.tensor.transpose(mi_ps[:, P * t:P * t + P], qk_rot[:, t, P * n:P * n + P], ident[:])
                last.then_inc(qkT_done, 1)

            def max_block(b, f, par):
                hh, kind, hp = f // 6, f % 6 // 2, f % 2
                if f >= 2:
                    pe.wait_ge(mx_read, FILLS * b + f - 1)
                if f == 0:
                    pe.wait_ge(stack, PER_STACK * (b + 1))
                rows = slice(64 * hp, 64 * hp + ROWS_QK)
                out = mx_ps[hp]

                def scores(at, qt, n, start, stop):
                    return nc.tensor.matmul(out[:, at:at + n * P], q_st[par][rows, hh, P * qt:P * qt + P],
                                            k_st[par][rows, hh, 0:n * P] if kind != DIAG else
                                            k_st[par][rows, hh, P * qt:P * qt + P], start=start, stop=stop)
                if kind == DIAG:
                    nc.tensor.matmul(out[:], ident_b[:], mask_b[:].rearrange("p t k -> p (t k)"),
                                     start=True, stop=False)
                    for w, t in enumerate(WTILE):
                        last = scores(P * w, t, 1, False, w == NT - 1)
                elif kind == OFF13:
                    scores(0, 1, 1, True, True)
                    last = scores(P, 3, 3, True, True)
                else:
                    last = scores(0, 2, 2, True, True)
                last.then_inc(mx_done, 1)

            def score_step(b, s, par):
                j, kt, pr = s // 8, s % 8 // 2, s % 2
                if s == 0:
                    pe.wait_ge(nm_dma, PER_NM * (b + 1))
                if s >= 2:
                    pe.wait_ge(ex_act, STEPS * b + s - 1)
                hh = 2 * j + pr
                for hp in range(2):
                    rows = slice(64 * hp, 64 * hp + ROWS_ALL)
                    last = nc.tensor.matmul(ex_ps[s % 2][:, hp, 0:S - P * kt], k_st[par][rows, hh, P * kt:P * kt + P],
                                            q_st[par][rows, hh, P * kt:], start=True, stop=True)
                last.then_inc(ex_done, 1)

            def pv(b, j, par):
                if j == 0:
                    pe.wait_ge(v_ev, NT * (b + 1))
                else:
                    pe.wait_ge(oT_ev, NG * b + j)
                for kt in range(NT):
                    pe.wait_ge(masked, 4 * NG * b + NT * j + kt + 1)
                    for g in range(G4):
                        last = nc.tensor.matmul(pv_ps[32 * g:32 * g + 32, P * kt:],
                                                v_sb[par][:, kt, G4 * j + g, :],
                                                prob[kt][j % 2 if kt < 2 else 0][:, g, :],
                                                start=kt == 0, stop=kt == NT - 1, skip_group_check=True)
                last.then_inc(pv_done, 1)

            def out_step(b, k):
                if k < 4:
                    if k == 0:
                        pe.wait_ge(oT_ev, NG * (b + 1))
                    else:
                        pe.wait_ge(attn_s, NT * b + k)
                    for j in range(NG):
                        last = nc.tensor.transpose(mi_ps[:, P * j:P * j + P], oT_sb[:, j, P * k:P * k + P], ident[:])
                    last.then_inc(o_done, 1)
                elif k < 6:
                    c = k - 4
                    if c == 0:
                        pe.wait_ge(attn_s, NT * (b + 1))
                    else:
                        pe.wait_ge(aT_ls, NC * b + c)
                    for t in range(NT):
                        last = nc.tensor.transpose(mi_ps[:, P * t:P * t + P], attn[:, t, P * c:P * c + P], ident[:])
                    last.then_inc(aT_done, 1)
                else:
                    u = k - 6
                    if u == 0:
                        pe.wait_ge(aT_ls, NC * (b + 1))
                    else:
                        pe.wait_ge(res, 2 * b + u)
                    for v in range(2):
                        tok = slice(P * (2 * u + v), P * (2 * u + v) + P)
                        terms = [(a, r, c) for c in range(NC) for a, r in ((aT_h, wo_h), (aT_h, wo_l), (aT_l, wo_h))]
                        for n, (a, r, c) in enumerate(terms):
                            last = nc.tensor.matmul(mi_ps[:, D * v:D * v + D], a[:, c, tok], r[:, c, :],
                                                    start=n == 0, stop=n == len(terms) - 1)
                    last.then_inc(wo_done, 1)

            def iteration(b, par, E=True, M=True, F=True):
                f = 0
                for s in range(STEPS):
                    if E:
                        score_step(b, s, par)
                    if M and s in T_AT:
                        n = T_AT[s]
                        if n == 0:
                            pe.wait_ge(rope, 3 * NT * (b + 2))
                            if not (isinstance(b, int) and b < 0):
                                pe.wait_ge(nmT_ev, b + 1)
                            else:
                                pe.wait_ge(qk_ev, NT)
                        else:
                            pe.wait_ge(qkT_l, PER_T * (b + 1) + n)
                        transpose_qk(b + 1, n)
                    if M and s in V_AT:
                        t = V_AT[s]
                        if t == 0:
                            pe.wait_ge(qkT_l, PER_T * (b + 2))
                        elif F:
                            pe.wait_ge(qk_ev, NT * (b + 2) + t)
                        else:
                            pe.wait_ge(v_ev, NT * (b + 1) + t)
                        project_v(b + 1, t, 1 - par)
                    if F and s in QK_AT:
                        t = QK_AT[s]
                        if t == 0:
                            pe.wait_ge(x_split, 2 * (b + 3))
                        pe.wait_ge(v_ev, NT * (b + 1) + t + 1)
                        project_qk(b + 2, t, par)
                    if E and s in PV_AT:
                        pv(b, PV_AT[s], par)
                    if M and s >= FILL_FROM:
                        max_block(b + 1, s - FILL_FROM, 1 - par)
                f = FILL_E
                if E:
                    pv(b, NG - 1, par)
                for k in range(8):
                    if E:
                        if k == 0:
                            if F:
                                pe.wait_ge(qk_ev, NT * (b + 3))
                            elif M:
                                pe.wait_ge(v_ev, NT * (b + 2))
                            else:
                                pe.wait_ge(nmT_ev, b + 1)
                        out_step(b, k)
                    if M:
                        for g in range(FILL_W):
                            max_block(b + 1, f + g, 1 - par)
                        f += FILL_W
                if M:
                    for g in range(FILL_LAST):
                        max_block(b + 1, f + g, 1 - par)
                    pe.wait_ge(nm, 4 * (b + 2))
                    if E:
                        pe.wait_ge(res, 2 * (b + 1))
                    else:
                        pe.wait_ge(qk_ev, 2 * NT)
                    for w, t in enumerate(WTILE):
                        last = nc.tensor.transpose(mi_ps[0:2 * H, P * t:P * t + P], nmax2[:, w, :], ident[:])
                    last.then_inc(nmT_done, 1)

            pe.wait_ge(idb_s, 1)
            pe.wait_ge(w_split, 6)
            pe.wait_ge(x_split, 2)
            pe.wait_ge(set_s, 4)
            for t in range(NT):
                if t:
                    pe.wait_ge(qk_ev, t)
                project_qk(0, t, 0)
            iteration(-1, 1, E=False)
            with pe.Fori(0, 3) as i:
                iteration(2 * i, 0)
                iteration(2 * i + 1, 1)
            iteration(6, 0, F=False)
            iteration(7, 1, M=False, F=False)


NK = I // P
HALVES = NK // 4
CMP = 9
DOWN_AFTER = {5: (0,), 6: (1,), 7: (2, 3)}
XT_AFTER = {1: 0, 3: 1}


def ffn_phase(nc, x1, wg, wu, wd, out):
    ctx = ExitStack()
    with ctx:
        def sb(name, shape, dt=f32):
            return ctx.enter_context(nc.sbuf_tensor(name, shape, dt))

        def sem(name):
            return ctx.enter_context(nc.semaphore(name))

        def ps(name, shape):
            return ctx.enter_context(nc.psum_tensor(name, shape, f32))

        wg_h, wg_l, wu_h, wu_l = [sb(n, [P, NC, NK, P], f32r) for n in ("wg_h", "wg_l", "wu_h", "wu_l")]
        wd_h, wd_l = [sb(n, [P, NK, D], f32r) for n in ("wd_h", "wd_l")]
        ident = sb("ident2", [P, P])
        mhalf = sb("mhalf2", [P, NT])
        xr = sb("xr", [P, NT, D])
        xh = [sb(f"x1h{i}", [P, NC, S], f32r) for i in range(2)]
        xl = [sb(f"x1l{i}", [P, NC, S], f32r) for i in range(2)]
        g_sb = sb("g_sb", [P, 2, S])
        h = [sb(f"h{i}", [P, 4, S]) for i in range(HALVES)]
        mag = sb("mag", [P, 4, S])
        ext = sb("ext", [P, 4, S])
        win = sb("win", [P, 2, 2, S], bf16)
        lim = sb("lim", [P, 4, S], bf16)
        hm_h = [sb(f"hm_h{i}", [P, NK, S], f32r) for i in range(2)]
        hm_l = [sb(f"hm_l{i}", [P, NK, S], f32r) for i in range(2)]
        y_sb = sb("y2_sb", [P, NT, D])
        stats = sb("stats2", [P, NT, 6])
        meanvar = sb("meanvar2", [P, NT, 2])
        vare = sb("vare2", [P, NT])
        rstd = sb("rstd2", [P, NT])

        g_ps = [ps(f"g_ps{i}", [P, S]) for i in range(2)]
        u_ps = [ps(f"u_ps{i}", [P, S]) for i in range(2)]
        d_ps = [ps(f"d_ps{i}", [P, S]) for i in range(2)]
        x_ps = ps("x_ps", [P, S])

        w_in = sem("f_w_in")
        w_high = sem("f_w_high")
        w_low = sem("f_w_low")
        const_s = sem("f_const")
        xr_in = sem("xr_in")
        y_in = sem("y_in")
        xt_done = sem("xt_done")
        xt_h = sem("xt_h")
        xt_l = sem("xt_l")
        g_done = sem("g_done")
        u_done = sem("u_done")
        silu_s = sem("silu_s")
        h_s = sem("h_s")
        mag_s = sem("mag_s")
        cmp_s = sem("cmp_s")
        hm_hs = sem("hm_hs")
        hm_ls = sem("hm_ls")
        d_done = sem("d_done")
        res = sem("f_res")
        stat = sem("f_stat")
        mv = sem("f_mv")
        rs = sem("f_rs")
        ln = sem("f_ln")
        y_out = sem("y_out")
        spare_pool, spare_dve, spare_sp = sem("f_spare_pool"), sem("f_spare_dve"), sem("f_spare_sp")

        block = ctx.enter_context(nc.Block())

        @block.sync
        def _(sp):
            for dst, src in ((h[0], wg), (h[1], wu)):
                sp.dma_start(dst[:].rearrange("p (c n) m -> p c (n m)", c=NC),
                             src.rearrange("(c p) i -> p c i", p=P)).then_inc(w_in, 16)
            sp.dma_start(mag[:].rearrange("p (a n) m -> p a (n m)", a=HALVES),
                         wd.rearrange("(a p j) d -> p a (j d)", a=HALVES, j=4)).then_inc(w_in, 16)

            def load_xr(b, first=False):
                if not first:
                    sp.wait_ge(xt_done, NC * b)
                sp.dma_start(xr[:], x1[b].rearrange("(t p) d -> p t d", p=P)).then_inc(xr_in, 16)

            def iteration(b, G=True, X=True, Dn=True):
                if X:
                    load_xr(b + 2)
                if Dn:
                    sp.dma_start(y_sb[:], x1[b].rearrange("(t p) d -> p t d", p=P)).then_inc(y_in, 16)
                    sp.wait_ge(ln, NT * (b + 1))
                    sp.dma_start(out[b].rearrange("(t p) d -> p t d", p=P), y_sb[:]).then_inc(y_out, 16)
                    wait_apart(sp, spare_sp, y_out, 16 * (b + 1))

            load_xr(0, first=True)
            iteration(-1, Dn=False)
            with sp.Fori(0, 3) as i:
                iteration(2 * i)
                iteration(2 * i + 1)
            iteration(6, X=False)
            iteration(7, G=False, X=False)

        @block.gpsimd
        def _(pool):
            nc.gpsimd.memset(ident[:], 0.0).then_inc(const_s, 1)
            nc.gpsimd.memset(mhalf[:], -0.5).then_inc(const_s, 1)
            pool.wait_ge(const_s, 2)
            nc.gpsimd.affine_select(out=ident[:], in_=ident[:], compare_op=ALU.not_equal, fill=1.0, base=0,
                                    pattern=[[-1, P]], channel_multiplier=1).then_inc(const_s, 1)

            def iteration(b):
                wait_apart(pool, spare_pool, mv, NT * (b + 1))
                nc.gpsimd.tensor_scalar(vare[:], meanvar[:, :, 1], EPS, None, ALU.add).then_inc(rs, 1)
                pool.wait_ge(rs, 2 * b + 1)
                nc.gpsimd.tensor_tensor(rstd[:], vare[:], mhalf[:], ALU.pow).then_inc(rs, 1)

            with pool.Fori(0, B) as b:
                iteration(b)

        @block.scalar
        def _(act):
            act.wait_ge(w_in, 3 * 16)
            for dst, raw in ((wg_h, h[0]), (wu_h, h[1])):
                v = raw[:].rearrange("p (c n) m -> p c (n m)", c=NC).rearrange("p c (a q j) -> p c a j q", a=HALVES, j=4)
                for c in range(NC):
                    for a in range(HALVES):
                        nc.scalar.activation(dst[:, c, 4 * a:4 * a + 4, :], v[:, c, a], ACT.Copy).then_inc(w_high, 1)
            nc.scalar.activation(wd_h[:].rearrange("p k d -> p (k d)"), mag[:].rearrange("p j n -> p (j n)"),
                                 ACT.Copy).then_inc(w_high, 1)

            def high_x(b, c, par):
                act.wait_ge(xt_done, NC * b + c + 1)
                nc.scalar.activation(xh[par][:, c, :], x_ps[:], ACT.Copy).then_inc(xt_h, 1)

            def silu(b, k):
                act.wait_ge(g_done, NK * b + k + 1)
                if not (isinstance(b, int) and b == 0 and k < 2):
                    act.wait_ge(h_s, NK * b + k - 1)
                nc.scalar.activation(g_sb[:, k % 2, :], g_ps[k % 2][:], ACT.Silu).then_inc(silu_s, 1)

            def magnitude(b, a):
                act.wait_ge(h_s, NK * b + 4 * a + 4)
                if not (isinstance(b, int) and b == 0 and a == 0):
                    act.wait_ge(cmp_s, CMP * (HALVES * b + a - 1) + 3)
                nc.scalar.activation(mag[:], h[a][:], ACT.Abs).then_inc(mag_s, 1)

            def high_hm(b, a, par):
                act.wait_ge(cmp_s, CMP * (HALVES * b + a + 1))
                nc.scalar.activation(hm_h[par][:, 4 * a:4 * a + 4, :], h[a][:], ACT.Copy).then_inc(hm_hs, 1)

            def iteration(b, par, G=True, X=True, Dn=True):
                if G:
                    for k in range(NK):
                        silu(b + 1, k)
                        if X and k in XT_AFTER:
                            high_x(b + 2, XT_AFTER[k], par)
                        if k == 3:
                            if Dn:
                                high_hm(b, 1, par)
                            magnitude(b + 1, 0)
                        if k == 7:
                            high_hm(b + 1, 0, 1 - par)
                            magnitude(b + 1, 1)
                else:
                    high_hm(b, 1, par)

            act.wait_ge(w_low, 3)
            for c in range(NC):
                high_x(0, c, 0)
            iteration(-1, 1, Dn=False)
            with act.Fori(0, 3) as i:
                iteration(2 * i, 0)
                iteration(2 * i + 1, 1)
            iteration(6, 0, X=False)
            iteration(7, 1, G=False, X=False)

        @block.vector
        def _(dve):
            for n, (dst, high, raw) in enumerate(((wg_l, wg_h, h[0]), (wu_l, wu_h, h[1]))):
                v = raw[:].rearrange("p (c n) m -> p c (n m)", c=NC).rearrange("p c (a q j) -> p c a j q", a=HALVES, j=4)
                dve.wait_ge(w_high, 4 * (n + 1))
                for c in range(NC):
                    for a in range(HALVES):
                        last = nc.vector.tensor_tensor(dst[:, c, 4 * a:4 * a + 4, :], v[:, c, a],
                                                       high[:, c, 4 * a:4 * a + 4, :].bitcast(f32), ALU.subtract)
                last.then_inc(w_low, 1)
            dve.wait_ge(w_high, 9)
            nc.vector.tensor_tensor(wd_l[:].rearrange("p k d -> p (k d)"), mag[:].rearrange("p j n -> p (j n)"),
                                    wd_h[:].rearrange("p k d -> p (k d)").bitcast(f32),
                                    ALU.subtract).then_inc(w_low, 1)

            def low_x(b, c, par):
                dve.wait_ge(xt_h, NC * b + c + 1)
                nc.vector.tensor_tensor(xl[par][:, c, :], x_ps[:], xh[par][:, c, :].bitcast(f32),
                                        ALU.subtract).then_inc(xt_l, 1)

            def product(b, k):
                dve.wait_ge(silu_s, NK * b + k + 1)
                dve.wait_ge(u_done, NK * b + k + 1)
                if k % 4 == 0 and not (isinstance(b, int) and b == 0):
                    dve.wait_ge(hm_ls, HALVES * b + k // 4 - 1)
                nc.vector.tensor_tensor(h[k // 4][:, k % 4, :], u_ps[k % 2][:], g_sb[:, k % 2, :],
                                        ALU.mult).then_inc(h_s, 1)

            def compare(b, a, q):
                base = CMP * (HALVES * b + a)
                m = mag[:].rearrange("p (r e) n -> p r e n", r=2)
                if q == 0:
                    dve.wait_ge(mag_s, HALVES * b + a + 1)
                    if not (isinstance(b, int) and b == 0 and a == 0):
                        dve.wait_ge(cmp_s, base)
                    nc.vector.tensor_tensor(ext[:, 1:3, :], m[:, :, 0], m[:, :, 1], ALU.max).then_inc(cmp_s, 1)
                    nc.vector.tensor_tensor(ext[:, 0:4:3, :], m[:, :, 0], m[:, :, 1], ALU.min).then_inc(cmp_s, 1)
                elif q == 1:
                    nc.vector.tensor_tensor(win[:, :, 0], m[:, :, 0], m[:, :, 1], ALU.is_ge).then_inc(cmp_s, 1)
                    dve.wait_ge(cmp_s, base + 3)
                    nc.vector.tensor_scalar(win[:, :, 1], win[:, :, 0], -1.0, 1.0, ALU.mult,
                                            ALU.add).then_inc(cmp_s, 1)
                    nc.vector.tensor_tensor(lim[:, 0:2, :], ext[:, 0:2, :], ext[:, 2:4, :],
                                            ALU.is_ge).then_inc(cmp_s, 1)
                    dve.wait_ge(cmp_s, base + 5)
                    nc.vector.tensor_scalar(lim[:, 2:4, :], lim[:, 0:2, :], -1.0, 1.0, ALU.mult,
                                            ALU.add).then_inc(cmp_s, 1)
                else:
                    dve.wait_ge(cmp_s, base + 6)
                    nc.vector.tensor_tensor(win[:], win[:], lim[:, 1:3, None, :].broadcast_to([P, 2, 2, S]),
                                            ALU.min).then_inc(cmp_s, 1)
                    dve.wait_ge(cmp_s, base + 7)
                    nc.vector.tensor_tensor(win[:], win[:], lim[:, 0:4:3, None, :].broadcast_to([P, 2, 2, S]),
                                            ALU.max).then_inc(cmp_s, 1)
                    dve.wait_ge(cmp_s, base + 8)
                    nc.vector.tensor_tensor(h[a][:], h[a][:], win[:].rearrange("p r e n -> p (r e) n"),
                                            ALU.mult).then_inc(cmp_s, 1)

            def low_hm(b, a, par):
                dve.wait_ge(hm_hs, HALVES * b + a + 1)
                nc.vector.tensor_tensor(hm_l[par][:, 4 * a:4 * a + 4, :], h[a][:],
                                        hm_h[par][:, 4 * a:4 * a + 4, :].bitcast(f32),
                                        ALU.subtract).then_inc(hm_ls, 1)

            def residual(b, t):
                dve.wait_ge(d_done, NT * b + t + 1)
                if t == 0:
                    dve.wait_ge(y_in, 16 * (b + 1))
                nc.vector.tensor_tensor(y_sb[:, t, :], d_ps[t % 2][:, 0:D], y_sb[:, t, :], ALU.add).then_inc(res, 1)

            def layer_norm(b):
                for t in range(NT):
                    dve.wait_ge(res, NT * b + t + 1)
                    nc.vector.bn_stats(stats[:, t, :], y_sb[:, t, :]).then_inc(stat, 1)
                for t in range(NT):
                    wait_apart(dve, spare_dve, stat, NT * b + t + 1)
                    nc.vector.bn_aggr(meanvar[:, t, :], stats[:, t, :]).then_inc(mv, 1)
                dve.wait_ge(rs, 2 * (b + 1))
                for t in range(NT):
                    nc.vector.tensor_scalar(y_sb[:, t, :], y_sb[:, t, :], meanvar[:, t, 0:1],
                                            rstd[:, t:t + 1], ALU.subtract, ALU.mult).then_inc(ln, 1)

            def iteration(b, par, G=True, X=True, Dn=True):
                if G:
                    for k in range(NK):
                        if k == 4 and Dn:
                            low_hm(b, 1, par)
                        product(b + 1, k)
                        if X and k in XT_AFTER:
                            low_x(b + 2, XT_AFTER[k], par)
                        if k < 3 and Dn:
                            compare(b, 1, k)
                        if 4 <= k < 7:
                            compare(b + 1, 0, k - 4)
                        if Dn and k in DOWN_AFTER:
                            for t in DOWN_AFTER[k]:
                                residual(b, t)
                    low_hm(b + 1, 0, 1 - par)
                else:
                    for q in range(3):
                        compare(b, 1, q)
                    low_hm(b, 1, par)
                    for t in range(NT):
                        residual(b, t)
                if Dn:
                    layer_norm(b)

            for c in range(NC):
                low_x(0, c, 0)
            iteration(-1, 1, Dn=False)
            with dve.Fori(0, 3) as i:
                iteration(2 * i, 0)
                iteration(2 * i + 1, 1)
            iteration(6, 0, X=False)
            iteration(7, 1, G=False, X=False)

        @block.tensor
        def _(pe):
            def project(b, k, par):
                first = isinstance(b, int) and b == 0 and k < 2
                if k == 0:
                    pe.wait_ge(xt_l, NC * (b + 1))
                for dst, wh, wl, read, inc in ((g_ps, wg_h, wg_l, silu_s, g_done), (u_ps, wu_h, wu_l, h_s, u_done)):
                    if not first:
                        pe.wait_ge(read, NK * b + k - 1)
                    n = 0
                    for c in range(NC):
                        for w, xx in ((wh, xh), (wh, xl), (wl, xh)):
                            last = nc.tensor.matmul(dst[k % 2][:], w[:, c, k, :], xx[par][:, c, :],
                                                    start=n == 0, stop=n == 3 * NC - 1)
                            n += 1
                    last.then_inc(inc, 1)

            def down(b, t, par):
                if t == 0:
                    pe.wait_ge(hm_ls, HALVES * (b + 1))
                if t >= 2:
                    pe.wait_ge(res, NT * b + t - 1)
                tok = slice(P * t, P * t + P)
                n = 0
                for k in range(NK):
                    for hm, w in ((hm_h, wd_h), (hm_h, wd_l), (hm_l, wd_h)):
                        last = nc.tensor.matmul(d_ps[t % 2][:, 0:D], hm[par][:, k, tok], w[:, k, :],
                                                start=n == 0, stop=n == 3 * NK - 1)
                        n += 1
                last.then_inc(d_done, 1)

            def transpose_x(b, c, first=False):
                if c == 0:
                    pe.wait_ge(xr_in, 16 * (b + 1))
                if not (first and c == 0):
                    pe.wait_ge(xt_l, NC * b + c)
                for t in range(NT):
                    last = nc.tensor.transpose(x_ps[:, P * t:P * t + P], xr[:, t, P * c:P * c + P], ident[:])
                last.then_inc(xt_done, 1)

            def iteration(b, par, G=True, X=True, Dn=True):
                if G:
                    for k in range(NK):
                        project(b + 1, k, 1 - par)
                        if X and k in XT_AFTER:
                            transpose_x(b + 2, XT_AFTER[k])
                        if Dn and k in DOWN_AFTER:
                            for t in DOWN_AFTER[k]:
                                down(b, t, par)
                else:
                    for t in range(NT):
                        down(b, t, par)

            pe.wait_ge(const_s, 3)
            for c in range(NC):
                transpose_x(0, c, first=True)
            pe.wait_ge(w_low, 3)
            iteration(-1, 1, Dn=False)
            with pe.Fori(0, 3) as i:
                iteration(2 * i, 0)
                iteration(2 * i + 1, 1)
            iteration(6, 0, X=False)
            iteration(7, 1, G=False, X=False)


def build(nc, x, xT, wqkvT, woT, wg, wu, wd, cos, sin, out):
    parts = nc.dram_tensor("parts", (2, 2, H, 2, DH, S), f32, kind="Internal").ap()
    maxima = nc.dram_tensor("maxima", (2 * H, S), f32, kind="Internal").ap()
    x1 = nc.dram_tensor("x1", (B, S, D), f32, kind="Internal").ap()
    attention_phase(nc, x, xT, wqkvT, woT, cos, sin, parts, maxima, x1)
    ffn_phase(nc, x1, wg, wu, wd, out)


def kernel(**inputs):
    import numpy as np
    import concourse.bacc as bacc
    from concourse.bass_utils import run_bass_kernel_spmd as run

    a = {k: np.asarray(v) for k, v in inputs.items()}
    x = a["L0_attn_x"]
    inv = (1.0 / 10000.0 ** (np.arange(0, DH, 2, dtype=np.float32) / np.float32(DH))).astype(np.float32)
    ang = np.outer(np.arange(S, dtype=np.float32), inv).astype(np.float32)
    c2 = np.repeat(np.cos(ang), 2, axis=1)
    s2 = np.stack([np.sin(ang), -np.sin(ang)], axis=-1).reshape(S, DH)
    cos = np.stack([c2 / 4, c2], axis=1).astype(np.float32)
    sin = np.stack([s2 / 4, s2], axis=1).astype(np.float32)
    arrays = {
        "x": x,
        "xT": np.ascontiguousarray(x.transpose(0, 2, 1)),
        "wqkvT": np.ascontiguousarray(np.concatenate([a["L0_attn_W" + n].T for n in "qkv"], axis=1)),
        "woT": np.ascontiguousarray(a["L0_attn_Wo"].T),
        "w_gate": a["L0_ffn_w_gate"], "w_up": a["L0_ffn_w_up"], "w_down": a["L0_ffn_w_down"],
        "cos": cos, "sin": sin,
    }
    nc = bacc.Bacc("TRN2", target_bir_lowering=False, num_devices=1)
    args = [nc.dram_tensor(n, v.shape, mybir.dt.from_np(v.dtype), kind="ExternalInput").ap()
            for n, v in arrays.items()]
    out = nc.dram_tensor("out", (B, S, D), f32, kind="ExternalOutput").ap()
    build(nc, *args, out)
    r = run(nc, [arrays], core_ids=[0])
    return r.results[0]["out"]
```

```python
from contextlib import ExitStack

import concourse.bass as bass
from concourse import mybir

f32 = mybir.dt.float32
f32r = mybir.dt.float32r
bf16 = mybir.dt.bfloat16
ALU = mybir.AluOpType
ACT = mybir.ActivationFunctionType
AX = mybir.AxisListType

P = 128
B, S, D = 8, 512, 256
H, DH = 16, 16
I = 1024
NT = S // P
NC = D // P
HH = H // 2
EPS = 1e-5
NEG = -1e30
G4 = 4
NG = H // G4

ROWS = 64
ROWS_QK = 3 * DH
ROWS_Q = 2 * DH + 2

WTILE = [0, 2, 1, 3]
WIN = 3
Q3, Q02, Q1 = range(3)
FILL_KIND = [(pair, hp, kind) for pair in range(2) for hp in range(2) for kind in (Q3, Q02)]
FILL_KIND[4:4] = [(0, 0, Q1)]
FILL_KIND.append((0, 1, Q1))
SLOT = {Q3: 9, Q02: 2, Q1: 6}
FILLS = len(FILL_KIND) * HH // 2

STEPS = H // 2 * NT
QK_AT = {1: 0, 2: 1, 4: 2, 7: 3}
T_AT = {20: 0, 22: 1, 24: 2, 26: 3}
PV_AT = {8 * (j + 1) + kt: (j, kt) for j in range(NG - 1) for kt in range(NT)}
OT_AT = {8 * (j + 1) + 4: j for j in range(NG - 1)}
FILL_FROM = 4
FILL_STEP = {s: range(FILLS * (s - FILL_FROM) // (STEPS - FILL_FROM), FILLS * (s - FILL_FROM + 1) // (STEPS - FILL_FROM))
             for s in range(FILL_FROM, STEPS)}
ROPE_MASK = 2
X_AFTER = 8


def wait_apart(engine, spare, semaphore, value):
    engine.wait_ge(semaphore, value)
    if not isinstance(value, int):
        engine.sem_inc(spare, 1)


def attention_phase(nc, x, xT, wqkvT, woT, cos, sin, q_parts, k_parts, maxima, x1):
    ctx = ExitStack()
    with ctx:
        def sb(name, shape, dt=f32):
            return ctx.enter_context(nc.sbuf_tensor(name, shape, dt))

        def sem(name):
            return ctx.enter_context(nc.semaphore(name))

        wqkv_h = sb("wqkv_h", [P, NC, 3 * D], f32r)
        wqkv_l = sb("wqkv_l", [P, NC, 3 * D], f32r)
        wo_h = sb("wo_h", [P, NC, D], f32r)
        wo_l = sb("wo_l", [P, NC, D], f32r)
        cos_sb = sb("cos_sb", [P, NT, 2, DH])
        sin_sb = sb("sin_sb", [P, NT, 2, DH])
        ident = sb("ident", [P, P])
        ident_b = sb("ident_b", [P, P], bf16)
        mask_b = sb("mask_b", [P, 2, P], bf16)
        mhalf = sb("mhalf", [P, NT])
        xT_sb = sb("xT_sb", [P, NC, S])
        xh = [sb(f"xh{i}", [P, NC, S], f32r) for i in range(2)]
        xl = [sb(f"xl{i}", [P, NC, S], f32r) for i in range(2)]
        qk_raw = sb("qk_raw", [P, 2, 2 * D])
        rope_s = sb("rope_s", [P, 2 * D])
        qk_rot = sb("qk_rot", [P, NT, 2 * D])
        part_h = sb("part_h", [P, 2, S], f32r)
        part_l = sb("part_l", [P, 2, S], f32r)
        q_st = [sb(f"q_st{i}", [P, HH, S], f32r) for i in range(2)]
        k_st = [sb(f"k_st{i}", [P, HH, S], f32r) for i in range(2)]
        v_sb = [sb(f"v_sb{i}", [P, NT, H, 32]) for i in range(2)]
        bmax = sb("bmax", [P, H, NT * WIN])
        nmax = sb("nmax", [P, H, NT])
        nmax_h = sb("nmax_h", [P, H, NT], f32r)
        nmax2 = sb("nmax2", [P, NT, 2 * H])
        nmaxT = sb("nmaxT", [2 * H, S], f32r)
        prob = [[sb(f"prob{kt}_{i}", [P, G4, S - P * kt]) for i in range(2 if kt < 2 else 1)]
                for kt in range(NT)]
        zeros = prob[3][0][0:DH].rearrange("p g n -> p (g n)")
        ones = prob[2][0][0:DH, 0:2, :].rearrange("p g n -> p (g n)")
        oT_sb = sb("oT_sb", [P, NG, S])
        rden = sb("rden", [P, NT, H, 1])
        attn = sb("attn", [P, NT, D])
        aT_h = sb("aT_h", [P, NC, S], f32r)
        aT_l = sb("aT_l", [P, NC, S], f32r)
        y_sb = sb("y_sb", [P, NT, D])
        stats = sb("stats", [P, NT, 6])
        meanvar = sb("meanvar", [P, NT, 2])
        vare = sb("vare", [P, NT])
        rstd = sb("rstd", [P, NT])

        mx_ps = [ctx.enter_context(nc.psum_tensor(f"mx_ps{i}", [P, S], f32)) for i in range(2)]
        ex_ps = [ctx.enter_context(nc.psum_tensor(f"ex_ps{i}", [P, 2, S], f32)) for i in range(2)]
        pv_ps = ctx.enter_context(nc.psum_tensor("pv_ps", [P, S], f32))
        mi_ps = ctx.enter_context(nc.psum_tensor("mi_ps", [P, S], f32))

        w_in = sem("w_in")
        w_split = sem("w_split")
        const_s = sem("const_s")
        idb_s = sem("idb_s")
        set_s = sem("set_s")
        pad_in = sem("pad_in")
        xT_in = sem("xT_in")
        x_in = sem("x_in")
        x_split = sem("x_split")
        qk_done = sem("qk_done")
        qk_ev = sem("qk_ev")
        v_done = sem("v_done")
        v_ev = sem("v_ev")
        rope = sem("rope")
        qkT_done = sem("qkT_done")
        qkT_h = sem("qkT_h")
        qkT_l = sem("qkT_l")
        spill = [sem(f"spill{i}") for i in range(2)]
        stack = sem("stack")
        mx_done = sem("mx_done")
        mx_read = sem("mx_read")
        nm = sem("nm")
        nmT_done = sem("nmT_done")
        nmT_ev = sem("nmT_ev")
        nm_spill = sem("nm_spill")
        nm_dma = sem("nm_dma")
        ex_done = sem("ex_done")
        ex_act = sem("ex_act")
        masked = sem("masked")
        pv_done = sem("pv_done")
        oT_ev = sem("oT_ev")
        o_done = sem("o_done")
        rden_s = sem("rden_s")
        attn_s = sem("attn_s")
        aT_done = sem("aT_done")
        aT_hs = sem("aT_hs")
        aT_ls = sem("aT_ls")
        wo_done = sem("wo_done")
        res = sem("res")
        stat = sem("stat")
        mv = sem("mv")
        rs = sem("rs")
        ln = sem("ln")
        x1_out = sem("x1_out")
        spare_pool, spare_dve = sem("spare_pool"), sem("spare_dve")
        PER_T, PER_SPILL, PER_STACK, PER_NM = 4, 4 * 16, 8 * 16, 2 * 16

        block = ctx.enter_context(nc.Block())

        @block.sync
        def _(sp):
            sp.dma_start(xT_sb[:], xT[0].rearrange("(c p) n -> p c n", p=P)).then_inc(xT_in, 16)
            sp.dma_start(prob[0][0][:, 0:NC, :].rearrange("p a b -> p (a b)")[:, 0:2 * S],
                         wqkvT.rearrange("(c p) n -> p c n", p=P)[:, :, 0:S]).then_inc(w_in, 16)
            sp.dma_start(prob[0][1][:, 0, :].rearrange("p (c n) -> p c n", c=NC),
                         wqkvT.rearrange("(c p) n -> p c n", p=P)[:, :, S:]).then_inc(w_in, 16)
            sp.dma_start(prob[0][1][:, 1, :].rearrange("p (c n) -> p c n", c=NC),
                         woT.rearrange("(c p) n -> p c n", p=P)).then_inc(w_in, 16)
            for dst, src in ((cos_sb, cos), (sin_sb, sin)):
                sp.dma_start(dst[:], src.rearrange("(t p) a d -> p t a d", p=P)).then_inc(w_in, 16)

            def load_xT(b):
                sp.wait_ge(x_split, 2 * b)
                sp.dma_start(xT_sb[:], xT[b].rearrange("(c p) n -> p c n", p=P)).then_inc(xT_in, 16)

            def spill_parts(b, n, par):
                dst = (q_parts, k_parts)[n // 2][par, 8 * (n % 2):8 * (n % 2) + 8]
                for src, there, e in ((part_h, qkT_h, (1, 0)[n // 2]), (part_l, qkT_l, (0, 1)[n // 2])):
                    sp.wait_ge(there, PER_T * b + n + 1)
                    sp.dma_start(dst[:, DH * e:DH * e + DH], src[:, n % 2, :].bitcast(f32)).then_inc(spill[n % 2], 16)

            def fill_stack(b, qk, par):
                for i in range(2):
                    sp.wait_ge(spill[i], PER_SPILL * b + 32 * (qk + 1))
                dst = (q_st, k_st)[qk][par]
                for hp in range(2):
                    src = (q_parts, k_parts)[qk][par].rearrange("(hh hp) r n -> hp r hh n", hp=2)[hp]
                    for to, at, n in (((0, 0, 2 * DH), (2 * DH, DH, DH + 2)),
                                      ((0, 0, DH), (DH, 0, 2 * DH)))[qk]:
                        lo = ROWS * hp + to
                        sp.dma_start(dst[lo:lo + n].bitcast(f32), src[at:at + n]).then_inc(stack, 16)

            def place_maxima(b, par):
                sp.wait_ge(nmT_ev, b + 1)
                sp.dma_start(maxima, nmaxT[:].bitcast(f32)).then_inc(nm_spill, 16)
                sp.wait_ge(nm_spill, 16 * (b + 1))
                for hp in range(2):
                    at = ROWS * hp + ROWS_QK
                    sp.dma_start(q_st[par][at:at + 2].bitcast(f32),
                                 maxima.rearrange("(hp hh e) n -> hp e hh n", hp=2, e=2)[hp]
                                 ).then_inc(nm_dma, 16)

            def load_x(b):
                sp.dma_start(y_sb[:], x[b].rearrange("(t p) d -> p t d", p=P)).then_inc(x_in, 16)

            def store_x1(b):
                sp.wait_ge(ln, NT * (b + 1))
                sp.dma_start(x1[b].rearrange("(t p) d -> p t d", p=P), y_sb[:]).then_inc(x1_out, 16)
                sp.wait_ge(x1_out, 16 * (b + 1))

            def iteration(b, par, E=True, M=True, F=True, X=True):
                if F:
                    for n in range(4):
                        spill_parts(b + 2, n, par)
                    if E:
                        sp.wait_ge(ex_done, STEPS * (b + 1))
                    fill_stack(b + 2, 0, par)
                if M:
                    place_maxima(b + 1, 1 - par)
                if F:
                    fill_stack(b + 2, 1, par)
                if X:
                    load_xT(b + 4)
                if E:
                    store_x1(b)
                if M:
                    load_x(b + 1)

            sp.wait_ge(set_s, 1)
            for par in range(2):
                sp.dma_start(q_parts[par, :, 2 * DH:].rearrange("h e n -> e h n"),
                             zeros[0:2, None, :].broadcast_to([2, H, S])).then_inc(pad_in, 16)
                for st, row in ((q_st, zeros), (k_st, ones)):
                    for hp in range(2):
                        lo = ROWS * hp + ROWS_QK
                        sp.dma_start(st[par][lo:lo + DH].bitcast(f32),
                                     row[:, None, :].broadcast_to([DH, HH, S])).then_inc(pad_in, 16)
            load_xT(1)
            sp.wait_ge(pad_in, 10 * 16)
            iteration(-2, 0, E=False, M=False)
            iteration(-1, 1, E=False)
            with sp.Fori(0, 2) as i:
                iteration(2 * i, 0)
                iteration(2 * i + 1, 1)
            iteration(4, 0, X=False)
            iteration(5, 1, X=False)
            iteration(6, 0, F=False, X=False)
            iteration(7, 1, M=False, F=False, X=False)

        def rope_op(engine, nc_engine, b, n):
            t, k = n // 3, n % 3
            raw = qk_raw[:, t % 2, :].rearrange("p (a h d) -> p a h d", a=2, h=H)
            rot = qk_rot[:, t, :]
            first = isinstance(b, int) and b == 0
            if k == 0:
                engine.wait_ge(qk_ev, NT * b + t + 1)
                if not first:
                    engine.wait_ge(qkT_done, PER_T * b)
                nc_engine.tensor_tensor(rot.rearrange("p (a h d) -> p a h d", a=2, h=H), raw,
                                        cos_sb[:, t, :, None, :].broadcast_to([P, 2, H, DH]),
                                        ALU.mult).then_inc(rope, 1)
            elif k == 1:
                if not (first and t == 0):
                    engine.wait_ge(rope, 3 * NT * b + n - 1)
                nc_engine.tensor_tensor(rope_s[:].rearrange("p (a h d) -> p a h d", a=2, h=H), raw,
                                        sin_sb[:, t, :, None, :].broadcast_to([P, 2, H, DH]),
                                        ALU.mult).then_inc(rope, 1)
            else:
                engine.wait_ge(rope, 3 * NT * b + n)
                nc_engine.tensor_tensor(rot.rearrange("p (n e) -> p n e", e=2),
                                        rot.rearrange("p (n e) -> p n e", e=2),
                                        rope_s[:].rearrange("p (n e) -> p n e", e=2)[:, :, ::-1],
                                        ALU.add).then_inc(rope, 1)

        def max_bank(b, f):
            if isinstance(b, int) and b == 0:
                return (mx_ps[0][:], mx_ps[1][:], ex_ps[0][:, 0, :], ex_ps[0][:, 1, :])[f % 4]
            return mx_ps[f % 2][:]

        @block.gpsimd
        def _(pool):
            nc.gpsimd.memset(ident[:], 0.0).then_inc(const_s, 1)
            nc.gpsimd.memset(mask_b[:], 0.0).then_inc(const_s, 1)
            nc.gpsimd.memset(mhalf[:], -0.5).then_inc(const_s, 1)
            pool.wait_ge(const_s, 3)
            nc.gpsimd.affine_select(out=ident[:], in_=ident[:], compare_op=ALU.not_equal, fill=1.0, base=0,
                                    pattern=[[-1, P]], channel_multiplier=1).then_inc(const_s, 1)
            nc.gpsimd.affine_select(out=mask_b[:], in_=mask_b[:], compare_op=ALU.is_ge, fill=NEG, base=0,
                                    pattern=[[0, 2], [-1, P]], channel_multiplier=1).then_inc(const_s, 1)
            pool.wait_ge(const_s, 5)
            nc.gpsimd.tensor_copy(ident_b[:], ident[:]).then_inc(idb_s, 1)

            def split_x(b, par):
                if not (isinstance(b, int) and b < 2):
                    pool.wait_ge(v_done, NT * (b - 1))
                wait_apart(pool, spare_pool, xT_in, 16 * (b + 1))
                nc.gpsimd.tensor_scalar(xh[par][:], xT_sb[:], 1.0, None, ALU.mult).then_inc(x_split, 1)
                pool.wait_ge(x_split, 2 * b + 1)
                nc.gpsimd.tensor_tensor(xl[par][:], xT_sb[:], xh[par][:].bitcast(f32),
                                        ALU.subtract).then_inc(x_split, 1)

            def mask(b, m):
                j, kt = m // NT, m % NT
                p = prob[kt][j % 2 if kt < 2 else 0]
                wait_apart(pool, spare_pool, ex_act, STEPS * b + 2 * m + 2)
                nc.gpsimd.affine_select(out=p[:, :, 0:P], in_=p[:, :, 0:P], compare_op=ALU.is_ge, fill=0.0,
                                        base=0, pattern=[[0, G4], [1, P]],
                                        channel_multiplier=-1).then_inc(masked, 1)

            def iteration(b, par, E=True, M=True, F=True, X=True):
                for m in range(4 * NG):
                    if E:
                        mask(b, m)
                    if F and ROPE_MASK * m < 3 * NT and not (isinstance(b, int) and b == -2):
                        for n in range(ROPE_MASK):
                            rope_op(pool, nc.gpsimd, b + 2, ROPE_MASK * m + n)
                    if X and m == X_AFTER:
                        split_x(b + 3, 1 - par)
                if E:
                    wait_apart(pool, spare_pool, mv, NT * (b + 1))
                    nc.gpsimd.tensor_scalar(vare[:], meanvar[:, :, 1], EPS, None, ALU.add).then_inc(rs, 1)
                    pool.wait_ge(rs, 2 * b + 1)
                    nc.gpsimd.tensor_tensor(rstd[:], vare[:], mhalf[:], ALU.pow).then_inc(rs, 1)

            split_x(0, 0)
            iteration(-2, 0, E=False, M=False)
            iteration(-1, 1, E=False)
            with pool.Fori(0, 2) as i:
                iteration(2 * i, 0)
                iteration(2 * i + 1, 1)
            iteration(4, 0)
            iteration(5, 1, X=False)
            iteration(6, 0, F=False, X=False)
            iteration(7, 1, M=False, F=False, X=False)

        @block.scalar
        def _(act):
            act.wait_ge(w_in, 5 * 16)
            raw_qk = prob[0][0][:, 0:NC, :]
            raw_v = prob[0][1][:, 0, :].rearrange("p (c n) -> p c n", c=NC)
            raw_o = prob[0][1][:, 1, :].rearrange("p (c n) -> p c n", c=NC)
            nc.scalar.activation(wqkv_h[:, :, 0:S], raw_qk, ACT.Copy).then_inc(w_split, 1)
            nc.scalar.activation(wqkv_h[:, :, S:], raw_v, ACT.Copy).then_inc(w_split, 1)
            nc.scalar.activation(wo_h[:], raw_o, ACT.Copy).then_inc(w_split, 1)

            def ev_qk(b, t):
                act.wait_ge(qk_done, NT * b + t + 1)
                if not (isinstance(b, int) and NT * b + t < 2):
                    act.wait_ge(rope, 3 * (NT * b + t - 1) - 1)
                nc.scalar.activation(qk_raw[:, t % 2, :], mi_ps[:], ACT.Copy).then_inc(qk_ev, 1)

            def ev_v(b, t, par):
                act.wait_ge(v_done, NT * b + t + 1)
                nc.scalar.activation(v_sb[par][:, t, :, 0:DH],
                                     ex_ps[1][:, t % 2, 0:D].rearrange("p (h d) -> p h d", h=H),
                                     ACT.Copy).then_inc(v_ev, 1)

            def high_qkT(b, n):
                act.wait_ge(qkT_done, PER_T * b + n + 1)
                if n >= 2:
                    act.wait_ge(spill[n % 2], PER_SPILL * b + 32)
                nc.scalar.activation(part_h[:, n % 2, :], mi_ps[:], ACT.Copy).then_inc(qkT_h, 1)

            def exp_step(b, s):
                j, kt, pr = s // 8, s % 8 // 2, s % 2
                p = prob[kt][j % 2 if kt < 2 else 0]
                act.wait_ge(ex_done, STEPS * b + s + 1)
                if kt < 2 and j >= 2:
                    act.wait_ge(pv_done, NT * (NG * b + j - 2) + kt + 1)
                if kt >= 2 and j >= 1:
                    act.wait_ge(pv_done, NT * (NG * b + j - 1) + kt + 1)
                n = S - P * kt
                nc.scalar.activation(p[:, 2 * pr:2 * pr + 2, :], ex_ps[s % 2][:, :, 0:n],
                                     ACT.Exp).then_inc(ex_act, 1)

            def ev_oT(b, j):
                act.wait_ge(pv_done, NT * (NG * b + j + 1))
                nc.scalar.activation(oT_sb[:, j, :], pv_ps[:], ACT.Copy).then_inc(oT_ev, 1)

            def iteration(b, par, E=True, M=True, F=True):
                for s in range(STEPS):
                    if E:
                        exp_step(b, s)
                    if F and s in QK_AT:
                        ev_qk(b + 2, QK_AT[s])
                    if F and s in T_AT:
                        high_qkT(b + 2, T_AT[s])
                    if E and s in OT_AT:
                        ev_oT(b, OT_AT[s])
                if E:
                    ev_oT(b, NG - 1)
                if M:
                    act.wait_ge(nmT_done, b + 2)
                    if not (isinstance(b, int) and b < 0):
                        act.wait_ge(nm_spill, 16 * (b + 1))
                    nc.scalar.activation(nmaxT[:], ex_ps[0][0:2 * H, 0, :], ACT.Copy).then_inc(nmT_ev, 1)
                if F:
                    for t in range(2):
                        ev_v(b + 2, t, par)
                if E:
                    for c in range(NC):
                        act.wait_ge(aT_done, NC * b + c + 1)
                        nc.scalar.activation(aT_h[:, c, :], mx_ps[c][:], ACT.Copy).then_inc(aT_hs, 1)
                if F:
                    for t in range(2, NT):
                        ev_v(b + 2, t, par)

            act.wait_ge(set_s, 4)
            iteration(-2, 0, E=False, M=False)
            iteration(-1, 1, E=False)
            with act.Fori(0, 3) as i:
                iteration(2 * i, 0)
                iteration(2 * i + 1, 1)
            iteration(6, 0, F=False)
            iteration(7, 1, M=False, F=False)

        @block.vector
        def _(dve):
            nc.vector.memset(zeros, 0.0)
            nc.vector.memset(ones, 1.0).then_inc(set_s, 1)
            for i in range(2):
                nc.vector.memset(v_sb[i][:], 1.0).then_inc(set_s, 1)
            nc.vector.memset(bmax[:], NEG).then_inc(set_s, 1)
            raw_qk = prob[0][0][:, 0:NC, :]
            raw_v = prob[0][1][:, 0, :].rearrange("p (c n) -> p c n", c=NC)
            raw_o = prob[0][1][:, 1, :].rearrange("p (c n) -> p c n", c=NC)
            dve.wait_ge(w_split, 3)
            nc.vector.tensor_tensor(wqkv_l[:, :, 0:S], raw_qk, wqkv_h[:, :, 0:S].bitcast(f32),
                                    ALU.subtract).then_inc(w_split, 1)
            nc.vector.tensor_tensor(wqkv_l[:, :, S:], raw_v, wqkv_h[:, :, S:].bitcast(f32),
                                    ALU.subtract).then_inc(w_split, 1)
            nc.vector.tensor_tensor(wo_l[:], raw_o, wo_h[:].bitcast(f32), ALU.subtract).then_inc(w_split, 1)

            def low_qkT(b, n):
                dve.wait_ge(qkT_h, PER_T * b + n + 1)
                nc.vector.tensor_tensor(part_l[:, n % 2, :], mi_ps[:], part_h[:, n % 2, :].bitcast(f32),
                                        ALU.subtract).then_inc(qkT_l, 1)

            def block_max(b, f):
                pair, hp, kind = FILL_KIND[f % len(FILL_KIND)]
                head = 2 * (f // len(FILL_KIND) * 2 + pair) + hp
                heads = slice(head, head + 3, 2) if kind == Q1 else slice(head, head + 1)
                n = {Q3: 1, Q02: 4, Q1: 2}[kind]
                dve.wait_ge(mx_done, FILLS * b + f + 1)
                nh = 2 if kind == Q1 else 1
                nc.vector.tensor_reduce(out=bmax[:, heads, SLOT[kind]:SLOT[kind] + n],
                                        in_=max_bank(b, f).rearrange("p (h n k) -> p h n k", h=nh, n=n),
                                        axis=AX.X, op=ALU.max).then_inc(mx_read, 1)

            def negate_max(b):
                dve.wait_ge(mx_read, FILLS * (b + 1))
                nc.vector.tensor_reduce(out=nmax[:], in_=bmax[:].rearrange("p h (w s) -> p h w s", w=NT),
                                        axis=AX.X, op=ALU.max, negate=True).then_inc(nm, 1)
                dve.wait_ge(nm, 4 * b + 1)
                nc.vector.tensor_copy(nmax_h[:], nmax[:]).then_inc(nm, 1)
                dve.wait_ge(nm, 4 * b + 2)
                view = nmax2[:].rearrange("p w (hp hh e) -> p e hp hh w", hp=2, e=2)
                src = [a.rearrange("p (hh hp) w -> p hp hh w", hp=2) for a in (nmax[:], nmax_h[:].bitcast(f32))]
                nc.vector.tensor_copy(view[:, 0], src[1]).then_inc(nm, 1)
                nc.vector.tensor_tensor(view[:, 1], src[0], src[1], ALU.subtract).then_inc(nm, 1)

            def normalise(b, t):
                o = (mx_ps[0], mx_ps[1], mi_ps, pv_ps)[t][:].rearrange("p (h c) -> p h c", h=H)
                dve.wait_ge(o_done, NT * b + t + 1)
                nc.vector.reciprocal(rden[:, t], o[:, :, DH:DH + 1]).then_inc(rden_s, 1)
                dve.wait_ge(rden_s, NT * b + t + 1)
                nc.vector.tensor_tensor(attn[:, t, :].rearrange("p (h d) -> p h d", h=H), o[:, :, 0:DH],
                                        rden[:, t].broadcast_to([P, H, DH]), ALU.mult).then_inc(attn_s, 1)

            def low_aT(b, c):
                dve.wait_ge(aT_hs, NC * b + c + 1)
                nc.vector.tensor_tensor(aT_l[:, c, :], mx_ps[c][:], aT_h[:, c, :].bitcast(f32),
                                        ALU.subtract).then_inc(aT_ls, 1)

            def residual(b, u):
                dve.wait_ge(wo_done, 2 * b + u + 1)
                if u == 0:
                    dve.wait_ge(x_in, 16 * (b + 1))
                y = y_sb[:, 2 * u:2 * u + 2, :]
                nc.vector.tensor_tensor(y, (mi_ps, pv_ps)[u][:].rearrange("p (t d) -> p t d", t=2), y,
                                        ALU.add).then_inc(res, 1)

            def iteration(b, par, E=True, M=True, F=True):
                if isinstance(b, int) and b == -2:
                    for n in range(3 * NT):
                        rope_op(dve, nc.vector, 0, n)
                for s in range(STEPS):
                    if M and s in FILL_STEP:
                        for f in FILL_STEP[s]:
                            block_max(b + 1, f)
                    if F and s in T_AT:
                        low_qkT(b + 2, T_AT[s])
                if M:
                    negate_max(b + 1)
                if E:
                    for t in range(NT):
                        normalise(b, t)
                    for c in range(NC):
                        low_aT(b, c)
                    for u in range(2):
                        residual(b, u)
                    for t in range(NT):
                        dve.wait_ge(res, 2 * (b + 1) + t // 2 + 1)
                        nc.vector.bn_stats(stats[:, t, :], y_sb[:, t, :]).then_inc(stat, 1)
                    for t in range(NT):
                        wait_apart(dve, spare_dve, stat, NT * b + t + 1)
                        nc.vector.bn_aggr(meanvar[:, t, :], stats[:, t, :]).then_inc(mv, 1)
                if E:
                    dve.wait_ge(rs, 2 * (b + 1))
                    for t in range(NT):
                        nc.vector.tensor_scalar(y_sb[:, t, :], y_sb[:, t, :], meanvar[:, t, 0:1],
                                                rstd[:, t:t + 1], ALU.subtract, ALU.mult).then_inc(ln, 1)

            dve.sem_inc(res, 2)
            dve.wait_ge(w_in, 5 * 16)
            iteration(-2, 0, E=False, M=False)
            iteration(-1, 1, E=False)
            with dve.Fori(0, 3) as i:
                iteration(2 * i, 0)
                iteration(2 * i + 1, 1)
            iteration(6, 0, F=False)
            iteration(7, 1, M=False, F=False)

        @block.tensor
        def _(pe):
            def product(out, lh, ll, rh, rl, chunks, inc):
                terms = [(a, r, c) for c in range(chunks) for a, r in ((lh, rh), (lh, rl), (ll, rh))]
                for n, (a, r, c) in enumerate(terms):
                    last = nc.tensor.matmul(out, a(c), r(c), start=n == 0, stop=n == len(terms) - 1)
                last.then_inc(inc, 1)

            def project_qk(b, t, par):
                tok = slice(P * t, P * t + P)
                product(mi_ps[:], lambda c: xh[par][:, c, tok], lambda c: xl[par][:, c, tok],
                        lambda c: wqkv_h[:, c, 0:2 * D], lambda c: wqkv_l[:, c, 0:2 * D], NC, qk_done)

            def project_v(b, t, par):
                tok = slice(P * t, P * t + P)
                product(ex_ps[1][:, t % 2, 0:D], lambda c: xh[par][:, c, tok], lambda c: xl[par][:, c, tok],
                        lambda c: wqkv_h[:, c, 2 * D:], lambda c: wqkv_l[:, c, 2 * D:], NC, v_done)

            def transpose_qk(b, n):
                for t in range(NT):
                    last = nc.tensor.transpose(mi_ps[:, P * t:P * t + P], qk_rot[:, t, P * n:P * n + P], ident[:])
                last.then_inc(qkT_done, 1)

            def max_block(b, f, par):
                pair, hp, kind = FILL_KIND[f % len(FILL_KIND)]
                hh = f // len(FILL_KIND) * 2 + pair
                rows = slice(ROWS * hp, ROWS * hp + ROWS)
                banks = 4 if isinstance(b, int) and b == 0 else 2
                if f >= banks:
                    pe.wait_ge(mx_read, FILLS * b + f - banks + 1)
                if f == 0:
                    pe.wait_ge(stack, PER_STACK * (b + 1))
                out = max_bank(b, f)

                def scores(at, hh, qt):
                    return nc.tensor.matmul(out[:, at:at + (qt + 1) * P], q_st[par][rows, hh, P * qt:P * qt + P],
                                            k_st[par][rows, hh, 0:(qt + 1) * P], start=False, stop=True,
                                            skip_group_check=True)

                first, step = {Q3: (3, 1), Q02: (0, 3), Q1: (1, 2)}[kind]
                diagonals = out.rearrange("p (n k) -> p n k", n=NT)[:, first:NT:step, :]
                nc.tensor.matmul(diagonals, ident_b[:], mask_b[:, 0:1 if kind == Q3 else 2, :], start=True,
                                 stop=False, skip_group_check=True)
                if kind == Q3:
                    last = scores(0, hh, 3)
                elif kind == Q02:
                    scores(0, hh, 0)
                    last = scores(P, hh, 2)
                else:
                    scores(0, hh, 1)
                    last = scores(2 * P, hh + 1, 1)
                last.then_inc(mx_done, 1)

            def score_step(b, s, par, M):
                j, kt, pr = s // 8, s % 8 // 2, s % 2
                if s == 0:
                    pe.wait_ge(nm_dma, PER_NM * (b + 1))
                if s >= 2:
                    pe.wait_ge(ex_act, STEPS * b + s - 1)
                if s == 1 and M:
                    pe.wait_ge(v_ev, NT * (b + 2))
                hh = 2 * j + pr
                for hp in range(2):
                    rows = slice(ROWS * hp, ROWS * hp + ROWS)
                    last = nc.tensor.matmul(ex_ps[s % 2][:, hp, 0:S - P * kt], k_st[par][rows, hh, P * kt:P * kt + P],
                                            q_st[par][rows, hh, P * kt:], start=True, stop=True)
                last.then_inc(ex_done, 1)

            def pv(b, j, kt, par):
                if kt == 0:
                    if j == 0:
                        pe.wait_ge(v_ev, NT * (b + 1))
                        pe.wait_ge(res, 2 * (b + 1))
                    else:
                        pe.wait_ge(oT_ev, NG * b + j)
                pe.wait_ge(masked, 4 * NG * b + NT * j + kt + 1)
                for g in range(G4):
                    last = nc.tensor.matmul(pv_ps[32 * g:32 * g + 32, P * kt:],
                                            v_sb[par][:, kt, G4 * j + g, :],
                                            prob[kt][j % 2 if kt < 2 else 0][:, g, :],
                                            start=kt == 0, stop=kt == NT - 1, skip_group_check=True)
                last.then_inc(pv_done, 1)

            def output_heads(b):
                pe.wait_ge(oT_ev, NG * (b + 1))
                for k in range(NT):
                    for j in range(NG):
                        last = nc.tensor.transpose((mx_ps[0], mx_ps[1], mi_ps, pv_ps)[k][:, P * j:P * j + P],
                                                   oT_sb[:, j, P * k:P * k + P], ident[:])
                    last.then_inc(o_done, 1)

            def output_transposes(b):
                pe.wait_ge(attn_s, NT * (b + 1))
                for c in range(NC):
                    for t in range(NT):
                        last = nc.tensor.transpose(mx_ps[c][:, P * t:P * t + P], attn[:, t, P * c:P * c + P], ident[:])
                    last.then_inc(aT_done, 1)

            def output_product(b):
                pe.wait_ge(aT_ls, NC * (b + 1))
                for u in range(2):
                    for v in range(2):
                        tok = slice(P * (2 * u + v), P * (2 * u + v) + P)
                        terms = [(a, r, c) for c in range(NC) for a, r in ((aT_h, wo_h), (aT_h, wo_l), (aT_l, wo_h))]
                        for n, (a, r, c) in enumerate(terms):
                            last = nc.tensor.matmul((mi_ps, pv_ps)[u][:, D * v:D * v + D], a[:, c, tok], r[:, c, :],
                                                    start=n == 0, stop=n == len(terms) - 1)
                    last.then_inc(wo_done, 1)

            def v_tiles(b, tiles, par, E):
                for t in tiles:
                    if t >= 2:
                        pe.wait_ge(v_ev, NT * b + t - 1)
                    elif E:
                        pe.wait_ge(ex_act, STEPS * (b - 1))
                    project_v(b, t, par)

            def stack_transposes(b, n):
                if n == 0:
                    pe.wait_ge(rope, 3 * NT * (b + 1))
                else:
                    pe.wait_ge(qkT_l, PER_T * b + n)
                transpose_qk(b, n)

            def transpose_maxima(b, E):
                if E:
                    pe.wait_ge(ex_act, STEPS * b - 1)
                pe.wait_ge(nm, 4 * (b + 1))
                for w, t in enumerate(WTILE):
                    last = nc.tensor.transpose(ex_ps[0][0:2 * H, 0, P * t:P * t + P], nmax2[:, w, :], ident[:])
                last.then_inc(nmT_done, 1)

            def iteration(b, par, E=True, M=True, F=True):
                for s in range(STEPS):
                    if E:
                        score_step(b, s, par, M)
                    fills = FILL_STEP.get(s, range(0)) if M else range(0)
                    for f in fills[:1]:
                        max_block(b + 1, f, 1 - par)
                    if F and s in QK_AT:
                        t = QK_AT[s]
                        if t == 0:
                            pe.wait_ge(x_split, 2 * (b + 3))
                            if E:
                                pe.wait_ge(res, 2 * (b + 1))
                            elif M:
                                pe.wait_ge(qkT_l, PER_T)
                        else:
                            pe.wait_ge(qk_ev, NT * (b + 2) + t)
                        project_qk(b + 2, t, par)
                    if F and s in T_AT:
                        stack_transposes(b + 2, T_AT[s])
                    if E and s in PV_AT:
                        pv(b, *PV_AT[s], par)
                    for f in fills[1:]:
                        max_block(b + 1, f, 1 - par)
                if E:
                    for kt in range(NT):
                        pv(b, NG - 1, kt, par)
                if M:
                    transpose_maxima(b + 1, E)
                if E:
                    if F:
                        pe.wait_ge(qkT_l, PER_T * (b + 3))
                    else:
                        pe.wait_ge(res, 2 * (b + 1))
                    output_heads(b)
                if F:
                    v_tiles(b + 2, range(2), par, E)
                if E:
                    output_transposes(b)
                if F:
                    v_tiles(b + 2, range(2, NT), par, E)
                if E:
                    output_product(b)

            pe.wait_ge(idb_s, 1)
            pe.wait_ge(w_split, 6)
            iteration(-2, 0, E=False, M=False)
            iteration(-1, 1, E=False)
            with pe.Fori(0, 3) as i:
                iteration(2 * i, 0)
                iteration(2 * i + 1, 1)
            iteration(6, 0, F=False)
            iteration(7, 1, M=False, F=False)


NK = I // P
HALVES = NK // 4
CMP = 10
HIGHS = 2 * HALVES
LN_STEPS = 4
DOWN_AFTER = {5: (0,), 6: (1,), 7: (2, 3)}
XT_AFTER = {1: 0, 5: 1}


def ffn_phase(nc, x1, wg, wu, wd, out):
    ctx = ExitStack()
    with ctx:
        def sb(name, shape, dt=f32):
            return ctx.enter_context(nc.sbuf_tensor(name, shape, dt))

        def sem(name):
            return ctx.enter_context(nc.semaphore(name))

        def ps(name, shape):
            return ctx.enter_context(nc.psum_tensor(name, shape, f32))

        wg_h, wg_l, wu_h, wu_l = [sb(n, [P, NC, NK, P], f32r) for n in ("wg_h", "wg_l", "wu_h", "wu_l")]
        wd_h, wd_l = [sb(n, [P, NK, D], f32r) for n in ("wd_h", "wd_l")]
        ident = sb("ident2", [P, P])
        mhalf = sb("mhalf2", [P, NT])
        xr = sb("xr", [P, NT, D])
        xh = [sb(f"x1h{i}", [P, NC, S], f32r) for i in range(2)]
        xl = [sb(f"x1l{i}", [P, NC, S], f32r) for i in range(2)]
        g_sb = sb("g_sb", [P, 2, S])
        h = [sb(f"h{i}", [P, 4, S]) for i in range(HALVES)]
        mag = sb("mag", [P, 4, S])
        ext = sb("ext", [P, 4, S])
        win = sb("win", [P, 2, 2, S], bf16)
        lim = sb("lim", [P, 4, S], bf16)
        hm_h = [sb(f"hm_h{i}", [P, NK, S], f32r) for i in range(2)]
        hm_l = [sb(f"hm_l{i}", [P, NK, S], f32r) for i in range(2)]
        y_sb = sb("y2_sb", [P, NT, D])
        stats = sb("stats2", [P, NT, 6])
        meanvar = sb("meanvar2", [P, NT, 2])
        vare = sb("vare2", [P, NT])
        rstd = sb("rstd2", [P, NT])
        mrstd = sb("mrstd", [P, NT])

        g_ps = [ps(f"g_ps{i}", [P, S]) for i in range(2)]
        u_ps = [ps(f"u_ps{i}", [P, S]) for i in range(2)]
        d_ps = [ps(f"d_ps{i}", [P, S]) for i in range(2)]
        x_ps = ps("x_ps", [P, S])

        w_in = sem("f_w_in")
        w_high = sem("f_w_high")
        w_low = sem("f_w_low")
        const_s = sem("f_const")
        xr_in = sem("xr_in")
        y_in = sem("y_in")
        xt_done = sem("xt_done")
        xt_h = sem("xt_h")
        xt_l = sem("xt_l")
        g_done = sem("g_done")
        u_done = sem("u_done")
        silu_s = sem("silu_s")
        h_s = sem("h_s")
        mag_s = sem("mag_s")
        cmp_s = sem("cmp_s")
        hm_hs = sem("hm_hs")
        hm_ls = [sem(f"hm_ls{a}") for a in range(HALVES)]
        d_done = sem("d_done")
        res = sem("f_res")
        stat = sem("f_stat")
        mv = sem("f_mv")
        rs = sem("f_rs")
        ln = sem("f_ln")
        y_out = sem("y_out")
        spare_pool, spare_dve, spare_sp = sem("f_spare_pool"), sem("f_spare_dve"), sem("f_spare_sp")

        block = ctx.enter_context(nc.Block())

        @block.sync
        def _(sp):
            for dst, src in ((h[0], wg), (h[1], wu)):
                sp.dma_start(dst[:].rearrange("p (c n) m -> p c (n m)", c=NC),
                             src.rearrange("(c p) i -> p c i", p=P)).then_inc(w_in, 16)
            sp.dma_start(mag[:].rearrange("p (a n) m -> p a (n m)", a=HALVES),
                         wd.rearrange("(a p j) d -> p a (j d)", a=HALVES, j=4)).then_inc(w_in, 16)

            def load_xr(b, first=False):
                if not first:
                    sp.wait_ge(xt_done, NC * b)
                sp.dma_start(xr[:], x1[b].rearrange("(t p) d -> p t d", p=P)).then_inc(xr_in, 16)

            def iteration(b, X=True, Dn=True):
                if Dn:
                    sp.dma_start(y_sb[:], x1[b].rearrange("(t p) d -> p t d", p=P)).then_inc(y_in, 16)
                if X:
                    load_xr(b + 3)
                if Dn:
                    sp.wait_ge(ln, NT * (b + 1))
                    sp.dma_start(out[b].rearrange("(t p) d -> p t d", p=P), y_sb[:]).then_inc(y_out, 16)
                    wait_apart(sp, spare_sp, y_out, 16 * (b + 1))

            load_xr(0, first=True)
            load_xr(1)
            iteration(-1, Dn=False)
            with sp.Fori(0, 2) as i:
                iteration(2 * i)
                iteration(2 * i + 1)
            iteration(4)
            for b in range(5, B):
                iteration(b, X=False)

        @block.gpsimd
        def _(pool):
            nc.gpsimd.memset(ident[:], 0.0).then_inc(const_s, 1)
            nc.gpsimd.memset(mhalf[:], -0.5).then_inc(const_s, 1)
            pool.wait_ge(const_s, 2)
            nc.gpsimd.affine_select(out=ident[:], in_=ident[:], compare_op=ALU.not_equal, fill=1.0, base=0,
                                    pattern=[[-1, P]], channel_multiplier=1).then_inc(const_s, 1)

            def low_hm(b, par):
                pool.wait_ge(hm_hs, HIGHS * b + 2)
                nc.gpsimd.tensor_tensor(hm_l[par][:, 0:4, :], h[0][:], hm_h[par][:, 0:4, :].bitcast(f32),
                                        ALU.subtract).then_inc(hm_ls[0], 1)

            def layer_norm(b):
                wait_apart(pool, spare_pool, mv, NT * (b + 1))
                nc.gpsimd.tensor_scalar(vare[:], meanvar[:, :, 1], EPS, None, ALU.add).then_inc(rs, 1)
                pool.wait_ge(rs, LN_STEPS * b + 1)
                nc.gpsimd.tensor_tensor(rstd[:], vare[:], mhalf[:], ALU.pow).then_inc(rs, 1)
                pool.wait_ge(rs, LN_STEPS * b + 2)
                nc.gpsimd.tensor_tensor(mrstd[:], meanvar[:, :, 0], rstd[:], ALU.mult).then_inc(rs, 1)
                wait_apart(pool, spare_pool, rs, LN_STEPS * b + 3)
                nc.gpsimd.tensor_scalar(mrstd[:], mrstd[:], -1.0, None, ALU.mult).then_inc(rs, 1)

            low_hm(0, 0)
            with pool.Fori(0, 3) as i:
                low_hm(2 * i + 1, 1)
                layer_norm(2 * i)
                low_hm(2 * i + 2, 0)
                layer_norm(2 * i + 1)
            low_hm(7, 1)
            layer_norm(6)
            layer_norm(7)

        @block.scalar
        def _(act):
            act.wait_ge(w_in, 3 * 16)
            for dst, raw in ((wg_h, h[0]), (wu_h, h[1])):
                v = raw[:].rearrange("p (c n) m -> p c (n m)", c=NC).rearrange("p c (a q j) -> p c a j q", a=HALVES, j=4)
                for c in range(NC):
                    for a in range(HALVES):
                        nc.scalar.activation(dst[:, c, 4 * a:4 * a + 4, :], v[:, c, a], ACT.Copy).then_inc(w_high, 1)
            nc.scalar.activation(wd_h[:].rearrange("p k d -> p (k d)"), mag[:].rearrange("p j n -> p (j n)"),
                                 ACT.Copy).then_inc(w_high, 1)

            def high_x(b, c, par):
                act.wait_ge(xt_done, NC * b + c + 1)
                nc.scalar.activation(xh[par][:, c, :], x_ps[:], ACT.Copy).then_inc(xt_h, 1)

            def silu(b, k):
                act.wait_ge(g_done, NK * b + k + 1)
                if not (isinstance(b, int) and b == 0 and k < 2):
                    act.wait_ge(h_s, NK * b + k - 1)
                nc.scalar.activation(g_sb[:, k % 2, :], g_ps[k % 2][:], ACT.Silu).then_inc(silu_s, 1)

            def magnitude(b, a):
                act.wait_ge(h_s, NK * b + 4 * a + 4)
                if not (isinstance(b, int) and b == 0 and a == 0):
                    act.wait_ge(cmp_s, CMP * (HALVES * b + a - 1) + 3)
                nc.scalar.activation(mag[:], h[a][:], ACT.Abs).then_inc(mag_s, 1)

            def high_hm(b, a, par):
                for r in range(2):
                    act.wait_ge(cmp_s, CMP * (HALVES * b + a) + 9 + r)
                    nc.scalar.activation(hm_h[par][:, 4 * a + 2 * r:4 * a + 2 * r + 2, :], h[a][:, 2 * r:2 * r + 2, :],
                                         ACT.Copy).then_inc(hm_hs, 1)

            def apply_norm(b):
                act.wait_ge(rs, LN_STEPS * (b + 1))
                for t in range(NT):
                    nc.scalar.activation(y_sb[:, t, :], y_sb[:, t, :], ACT.Identity, bias=mrstd[:, t:t + 1],
                                         scale=rstd[:, t:t + 1]).then_inc(ln, 1)

            def iteration(b, par, G=True, X=True, Dn=True, norm=True):
                if G:
                    for k in range(NK):
                        silu(b + 1, k)
                        if norm and k == 2:
                            apply_norm(b - 1)
                        if X and k in XT_AFTER:
                            high_x(b + 2, XT_AFTER[k], par)
                        if k == 3 and Dn:
                            high_hm(b, 1, par)
                        if k == 4:
                            magnitude(b + 1, 0)
                        if k == 7:
                            high_hm(b + 1, 0, 1 - par)
                            magnitude(b + 1, 1)
                else:
                    high_hm(b, 1, par)
                    apply_norm(b - 1)

            act.wait_ge(w_low, 3)
            for c in range(NC):
                high_x(0, c, 0)
            iteration(-1, 1, Dn=False, norm=False)
            iteration(0, 0, norm=False)
            with act.Fori(0, 2) as i:
                iteration(2 * i + 1, 1)
                iteration(2 * i + 2, 0)
            iteration(5, 1)
            iteration(6, 0, X=False)
            iteration(7, 1, G=False, X=False)
            apply_norm(7)

        @block.vector
        def _(dve):
            for n, (dst, high, raw) in enumerate(((wg_l, wg_h, h[0]), (wu_l, wu_h, h[1]))):
                v = raw[:].rearrange("p (c n) m -> p c (n m)", c=NC).rearrange("p c (a q j) -> p c a j q", a=HALVES, j=4)
                dve.wait_ge(w_high, 4 * (n + 1))
                for c in range(NC):
                    for a in range(HALVES):
                        last = nc.vector.tensor_tensor(dst[:, c, 4 * a:4 * a + 4, :], v[:, c, a],
                                                       high[:, c, 4 * a:4 * a + 4, :].bitcast(f32), ALU.subtract)
                last.then_inc(w_low, 1)
            dve.wait_ge(w_high, 9)
            nc.vector.tensor_tensor(wd_l[:].rearrange("p k d -> p (k d)"), mag[:].rearrange("p j n -> p (j n)"),
                                    wd_h[:].rearrange("p k d -> p (k d)").bitcast(f32),
                                    ALU.subtract).then_inc(w_low, 1)

            def low_x(b, c, par):
                dve.wait_ge(xt_h, NC * b + c + 1)
                nc.vector.tensor_tensor(xl[par][:, c, :], x_ps[:], xh[par][:, c, :].bitcast(f32),
                                        ALU.subtract).then_inc(xt_l, 1)

            def product(b, k):
                dve.wait_ge(silu_s, NK * b + k + 1)
                dve.wait_ge(u_done, NK * b + k + 1)
                if k % 4 == 0 and not (isinstance(b, int) and b == 0):
                    dve.wait_ge(hm_ls[k // 4], (1 + k // 4) * b)
                nc.vector.tensor_tensor(h[k // 4][:, k % 4, :], u_ps[k % 2][:], g_sb[:, k % 2, :],
                                        ALU.mult).then_inc(h_s, 1)

            def compare(b, a, q):
                base = CMP * (HALVES * b + a)
                m = mag[:].rearrange("p (r e) n -> p r e n", r=2)
                if q == 0:
                    dve.wait_ge(mag_s, HALVES * b + a + 1)
                    if not (isinstance(b, int) and b == 0 and a == 0):
                        dve.wait_ge(cmp_s, base)
                    nc.vector.tensor_tensor(ext[:, 1:3, :], m[:, :, 0], m[:, :, 1], ALU.max).then_inc(cmp_s, 1)
                    nc.vector.tensor_tensor(ext[:, 0:4:3, :], m[:, :, 0], m[:, :, 1], ALU.min).then_inc(cmp_s, 1)
                elif q == 1:
                    nc.vector.tensor_tensor(win[:, :, 0], m[:, :, 0], m[:, :, 1], ALU.is_ge).then_inc(cmp_s, 1)
                    dve.wait_ge(cmp_s, base + 3)
                    nc.vector.tensor_scalar(win[:, :, 1], win[:, :, 0], -1.0, 1.0, ALU.mult,
                                            ALU.add).then_inc(cmp_s, 1)
                    nc.vector.tensor_tensor(lim[:, 0:2, :], ext[:, 0:2, :], ext[:, 2:4, :],
                                            ALU.is_ge).then_inc(cmp_s, 1)
                    dve.wait_ge(cmp_s, base + 5)
                    nc.vector.tensor_scalar(lim[:, 2:4, :], lim[:, 0:2, :], -1.0, 1.0, ALU.mult,
                                            ALU.add).then_inc(cmp_s, 1)
                elif q == 2:
                    dve.wait_ge(cmp_s, base + 6)
                    nc.vector.tensor_tensor(win[:], win[:], lim[:, 1:3, None, :].broadcast_to([P, 2, 2, S]),
                                            ALU.min).then_inc(cmp_s, 1)
                    dve.wait_ge(cmp_s, base + 7)
                    nc.vector.tensor_tensor(win[:], win[:], lim[:, 0:4:3, None, :].broadcast_to([P, 2, 2, S]),
                                            ALU.max).then_inc(cmp_s, 1)
                else:
                    dve.wait_ge(cmp_s, base + 8)
                    for r in range(2):
                        nc.vector.tensor_tensor(h[a][:, 2 * r:2 * r + 2, :], h[a][:, 2 * r:2 * r + 2, :],
                                                win[:, r], ALU.mult).then_inc(cmp_s, 1)

            def low_hm(b, par):
                for r in range(2):
                    k = 4 + 2 * r
                    dve.wait_ge(hm_hs, HIGHS * b + 3 + r)
                    nc.vector.tensor_tensor(hm_l[par][:, k:k + 2, :], h[1][:, 2 * r:2 * r + 2, :],
                                            hm_h[par][:, k:k + 2, :].bitcast(f32), ALU.subtract).then_inc(hm_ls[1], 1)

            def residual(b, t):
                dve.wait_ge(d_done, NT * b + t + 1)
                if t == 0:
                    dve.wait_ge(y_in, 16 * (b + 1))
                nc.vector.tensor_tensor(y_sb[:, t, :], d_ps[t % 2][:, 0:D], y_sb[:, t, :], ALU.add).then_inc(res, 1)

            def statistics(b, t):
                dve.wait_ge(res, NT * b + t + 1)
                nc.vector.bn_stats(stats[:, t, :], y_sb[:, t, :]).then_inc(stat, 1)

            def residual_and_statistics(b, t):
                residual(b, t)
                if t:
                    statistics(b, t - 1)
                if t == NT - 1:
                    statistics(b, t)
                    for n in range(NT):
                        wait_apart(dve, spare_dve, stat, NT * b + n + 1)
                        nc.vector.bn_aggr(meanvar[:, n, :], stats[:, n, :]).then_inc(mv, 1)

            def iteration(b, par, G=True, X=True, Dn=True):
                if G:
                    for k in range(NK):
                        if k == 4 and Dn:
                            low_hm(b, par)
                        product(b + 1, k)
                        if X and k in XT_AFTER:
                            low_x(b + 2, XT_AFTER[k], par)
                        if k < 3 and Dn:
                            compare(b, 1, k + 1)
                        if k >= 4:
                            compare(b + 1, 0, k - 4)
                        if Dn and k in DOWN_AFTER:
                            for t in DOWN_AFTER[k]:
                                residual_and_statistics(b, t)
                    compare(b + 1, 1, 0)
                else:
                    for q in range(1, 4):
                        compare(b, 1, q)
                    low_hm(b, par)
                    for t in range(NT):
                        residual_and_statistics(b, t)

            for c in range(NC):
                low_x(0, c, 0)
            iteration(-1, 1, Dn=False)
            with dve.Fori(0, 3) as i:
                iteration(2 * i, 0)
                iteration(2 * i + 1, 1)
            iteration(6, 0, X=False)
            iteration(7, 1, G=False, X=False)

        @block.tensor
        def _(pe):
            def project(b, k, par):
                first = isinstance(b, int) and b == 0 and k < 2
                if k == 0:
                    pe.wait_ge(xt_l, NC * (b + 1))
                for dst, wh, wl, read, inc in ((g_ps, wg_h, wg_l, silu_s, g_done), (u_ps, wu_h, wu_l, h_s, u_done)):
                    if not first:
                        pe.wait_ge(read, NK * b + k - 1)
                    n = 0
                    for c in range(NC):
                        for w, xx in ((wh, xh), (wh, xl), (wl, xh)):
                            last = nc.tensor.matmul(dst[k % 2][:], w[:, c, k, :], xx[par][:, c, :],
                                                    start=n == 0, stop=n == 3 * NC - 1)
                            n += 1
                    last.then_inc(inc, 1)

            def down(b, t, par):
                if t == 0:
                    for a in range(HALVES):
                        pe.wait_ge(hm_ls[a], (1 + a) * (b + 1))
                if t >= 2:
                    pe.wait_ge(res, NT * b + t - 1)
                tok = slice(P * t, P * t + P)
                n = 0
                for k in range(NK):
                    for hm, w in ((hm_h, wd_h), (hm_h, wd_l), (hm_l, wd_h)):
                        last = nc.tensor.matmul(d_ps[t % 2][:, 0:D], hm[par][:, k, tok], w[:, k, :],
                                                start=n == 0, stop=n == 3 * NK - 1)
                        n += 1
                last.then_inc(d_done, 1)

            def transpose_x(b, c, first=False):
                if c == 0:
                    pe.wait_ge(xr_in, 16 * (b + 1))
                if not (first and c == 0):
                    pe.wait_ge(xt_l, NC * b + c)
                for t in range(NT):
                    last = nc.tensor.transpose(x_ps[:, P * t:P * t + P], xr[:, t, P * c:P * c + P], ident[:])
                last.then_inc(xt_done, 1)

            def iteration(b, par, G=True, X=True, Dn=True):
                if G:
                    for k in range(NK):
                        project(b + 1, k, 1 - par)
                        if X and k in XT_AFTER:
                            transpose_x(b + 2, XT_AFTER[k])
                        if Dn and k in DOWN_AFTER:
                            for t in DOWN_AFTER[k]:
                                down(b, t, par)
                else:
                    for t in range(NT):
                        down(b, t, par)

            pe.wait_ge(const_s, 3)
            for c in range(NC):
                transpose_x(0, c, first=True)
            pe.wait_ge(w_low, 3)
            iteration(-1, 1, Dn=False)
            with pe.Fori(0, 3) as i:
                iteration(2 * i, 0)
                iteration(2 * i + 1, 1)
            iteration(6, 0, X=False)
            iteration(7, 1, G=False, X=False)


def build(nc, x, xT, wqkvT, woT, wg, wu, wd, cos, sin, out):
    q_parts = nc.dram_tensor("q_parts", (2, H, ROWS_Q, S), f32, kind="Internal").ap()
    k_parts = nc.dram_tensor("k_parts", (2, H, 2 * DH, S), f32, kind="Internal").ap()
    maxima = nc.dram_tensor("maxima", (2 * H, S), f32, kind="Internal").ap()
    x1 = nc.dram_tensor("x1", (B, S, D), f32, kind="Internal").ap()
    attention_phase(nc, x, xT, wqkvT, woT, cos, sin, q_parts, k_parts, maxima, x1)
    ffn_phase(nc, x1, wg, wu, wd, out)


def kernel(**inputs):
    import numpy as np
    import concourse.bacc as bacc
    from concourse.bass_utils import run_bass_kernel_spmd as run

    a = {k: np.asarray(v) for k, v in inputs.items()}
    x = a["L0_attn_x"]
    inv = (1.0 / 10000.0 ** (np.arange(0, DH, 2, dtype=np.float32) / np.float32(DH))).astype(np.float32)
    ang = np.outer(np.arange(S, dtype=np.float32), inv).astype(np.float32)
    c2 = np.repeat(np.cos(ang), 2, axis=1)
    s2 = np.stack([np.sin(ang), -np.sin(ang)], axis=-1).reshape(S, DH)
    cos = np.stack([c2 / 4, c2], axis=1).astype(np.float32)
    sin = np.stack([s2 / 4, s2], axis=1).astype(np.float32)
    arrays = {
        "x": x,
        "xT": np.ascontiguousarray(x.transpose(0, 2, 1)),
        "wqkvT": np.ascontiguousarray(np.concatenate([a["L0_attn_W" + n].T for n in "qkv"], axis=1)),
        "woT": np.ascontiguousarray(a["L0_attn_Wo"].T),
        "w_gate": a["L0_ffn_w_gate"], "w_up": a["L0_ffn_w_up"], "w_down": a["L0_ffn_w_down"],
        "cos": cos, "sin": sin,
    }
    nc = bacc.Bacc("TRN2", target_bir_lowering=False, num_devices=1)
    args = [nc.dram_tensor(n, v.shape, mybir.dt.from_np(v.dtype), kind="ExternalInput").ap()
            for n, v in arrays.items()]
    out = nc.dram_tensor("out", (B, S, D), f32, kind="ExternalOutput").ap()
    build(nc, *args, out)
    r = run(nc, [arrays], core_ids=[0])
    return r.results[0]["out"]
```

```python
from contextlib import ExitStack

import concourse.bass as bass
from concourse import mybir

f32 = mybir.dt.float32
f32r = mybir.dt.float32r
bf16 = mybir.dt.bfloat16
ALU = mybir.AluOpType
ACT = mybir.ActivationFunctionType
AX = mybir.AxisListType

P = 128
B, S, D = 8, 512, 256
H, DH = 16, 16
I = 1024
NT = S // P
NC = D // P
HH = H // 2
EPS = 1e-5
NEG = -1e30
G4 = 4
NG = H // G4

ROWS = 64
ROWS_QK = 3 * DH
ROWS_Q = 2 * DH + 2

WTILE = [0, 2, 1, 3]
WIN = 3
Q3, Q02, Q1 = range(3)
FILL_KIND = [(pair, hp, kind) for pair in range(2) for hp in range(2) for kind in (Q3, Q02)]
FILL_KIND[4:4] = [(0, 0, Q1)]
FILL_KIND.append((0, 1, Q1))
SLOT = {Q3: 9, Q02: 2, Q1: 6}
FILLS = len(FILL_KIND) * HH // 2

STEPS = H // 2 * NT
QK_AT = {1: 0, 2: 1, 4: 2, 7: 3}
T_AT = {20: 0, 22: 1, 24: 2, 26: 3}
PV_AT = {8 * (j + 1) + kt: (j, kt) for j in range(NG - 1) for kt in range(NT)}
OT_AT = {8 * (j + 1) + 4: j for j in range(NG - 1)}
FILL_FROM = 2
FILL_STEP = {s: range(FILLS * (s - FILL_FROM) // (STEPS - FILL_FROM), FILLS * (s - FILL_FROM + 1) // (STEPS - FILL_FROM))
             for s in range(FILL_FROM, STEPS)}
ROPE_MASK = 2
X_AFTER = 8
WARM_END = 28
WARM_6 = 1
WARM_7 = 1


def wait_apart(engine, spare, semaphore, value):
    engine.wait_ge(semaphore, value)
    if not isinstance(value, int):
        engine.sem_inc(spare, 1)


class Shared:

    def __init__(self, nc, ctx):
        def sb(name, shape, dt=f32):
            return ctx.enter_context(nc.sbuf_tensor(name, shape, dt))

        def stack(pair):
            flat = pair[:].rearrange("p l c k q -> p (l c k q)")
            return flat.rearrange("p (hh n) -> p hh n", n=S)

        self.v_sb0 = sb("v_sb0", [P, NT, H, 32])
        self.qk_rot = sb("qk_rot", [P, NT, 2 * D])
        self.xT_sb = sb("xT_sb", [P, NC, S])
        self.qk_raw = sb("qk_raw", [P, 2, 2 * D])
        self.ident = sb("ident", [P, P])
        self.y_sb = sb("y_sb", [P, NT, D])
        self.x1_out = ctx.enter_context(nc.semaphore("x1_out"))
        self.gate, self.up = [sb(n, [P, 2, NC, NK, P], f32r) for n in ("w_gate_parts", "w_up_parts")]
        self.q_st0, self.k_st0 = stack(self.gate), stack(self.up)
        self.xh0 = sb("xh0", [P, NC, S], f32r)
        self.weights_in = ctx.enter_context(nc.semaphore("ffn_weights_in"))
        self.xr_in = ctx.enter_context(nc.semaphore("xr_in"))
        self.w_parts = ctx.enter_context(nc.semaphore("w_parts"))

    def xr(self):
        return self.xh0[:].rearrange("p c n -> p (c n)").rearrange("p (t d) -> p t d", d=D).bitcast(f32)

    def halves(self):
        return [self.v_sb0[:].rearrange("p t h c -> p t (h c)"), self.qk_rot[:]]

    def raw_weights(self):
        gate, up = [h.rearrange("p (c n) m -> p c (n m)", c=NC) for h in self.halves()]
        down = [t[:].rearrange("p a n -> p (a n)") for t in (self.xT_sb, self.qk_raw)]
        return [gate, up, *down]


def attention_phase(nc, x, xT, wqkvT, woT, cos, sin, ffn_weights, q_parts, k_parts, maxima, x1, shared):
    ctx = ExitStack()
    with ctx:
        def sb(name, shape, dt=f32):
            return ctx.enter_context(nc.sbuf_tensor(name, shape, dt))

        def sem(name):
            return ctx.enter_context(nc.semaphore(name))

        wqkv_h = sb("wqkv_h", [P, NC, 3 * D], f32r)
        wqkv_l = sb("wqkv_l", [P, NC, 3 * D], f32r)
        wo_h = sb("wo_h", [P, NC, D], f32r)
        wo_l = sb("wo_l", [P, NC, D], f32r)
        cos_sb = sb("cos_sb", [P, NT, 2, DH])
        sin_sb = sb("sin_sb", [P, NT, 2, DH])
        ident = shared.ident
        ident_b = sb("ident_b", [P, P], bf16)
        mask_b = sb("mask_b", [P, 2, P], bf16)
        mhalf = sb("mhalf", [P, NT])
        xT_sb = shared.xT_sb
        xh = [shared.xh0, sb("xh1", [P, NC, S], f32r)]
        xl = [sb(f"xl{i}", [P, NC, S], f32r) for i in range(2)]
        qk_raw = shared.qk_raw
        rope_s = sb("rope_s", [P, 2 * D])
        qk_rot = shared.qk_rot
        part_h = sb("part_h", [P, 2, S], f32r)
        part_l = sb("part_l", [P, 2, S], f32r)
        q_st = [shared.q_st0, sb("q_st1", [P, HH, S], f32r)[:]]
        k_st = [shared.k_st0, sb("k_st1", [P, HH, S], f32r)[:]]
        v_sb = [shared.v_sb0, sb("v_sb1", [P, NT, H, 32])]
        bmax = sb("bmax", [P, H, NT * WIN])
        nmax = sb("nmax", [P, H, NT])
        nmax_h = sb("nmax_h", [P, H, NT], f32r)
        nmax2 = sb("nmax2", [P, NT, 2 * H])
        nmaxT = sb("nmaxT", [2 * H, S], f32r)
        prob = [[sb(f"prob{kt}_{i}", [P, G4, S - P * kt]) for i in range(2 if kt < 2 else 1)]
                for kt in range(NT)]
        zeros = prob[3][0][0:DH].rearrange("p g n -> p (g n)")
        ones = prob[2][0][0:DH, 0:2, :].rearrange("p g n -> p (g n)")
        oT_sb = sb("oT_sb", [P, NG, S])
        rden = sb("rden", [P, NT, H, 1])
        attn = sb("attn", [P, NT, D])
        aT_h = sb("aT_h", [P, NC, S], f32r)
        aT_l = sb("aT_l", [P, NC, S], f32r)
        y_sb = shared.y_sb
        stats = sb("stats", [P, NT, 6])
        meanvar = sb("meanvar", [P, NT, 2])
        vare = sb("vare", [P, NT])
        rstd = sb("rstd", [P, NT])

        mx_ps = [ctx.enter_context(nc.psum_tensor(f"mx_ps{i}", [P, S], f32)) for i in range(2)]
        ex_ps = [ctx.enter_context(nc.psum_tensor(f"ex_ps{i}", [P, 2, S], f32)) for i in range(2)]
        pv_ps = ctx.enter_context(nc.psum_tensor("pv_ps", [P, S], f32))
        mi_ps = ctx.enter_context(nc.psum_tensor("mi_ps", [P, S], f32))

        w_in = sem("w_in")
        w_split = sem("w_split")
        const_s = sem("const_s")
        idb_s = sem("idb_s")
        set_s = sem("set_s")
        pad_in = sem("pad_in")
        xT_in = sem("xT_in")
        x_in = sem("x_in")
        x_split = sem("x_split")
        qk_done = sem("qk_done")
        qk_ev = sem("qk_ev")
        v_done = sem("v_done")
        v_ev = sem("v_ev")
        rope = sem("rope")
        qkT_done = sem("qkT_done")
        qkT_h = sem("qkT_h")
        qkT_l = sem("qkT_l")
        spill = [sem(f"spill{i}") for i in range(2)]
        stack = sem("stack")
        mx_done = sem("mx_done")
        mx_read = sem("mx_read")
        nm = sem("nm")
        nmT_done = sem("nmT_done")
        nmT_ev = sem("nmT_ev")
        nm_spill = sem("nm_spill")
        nm_dma = sem("nm_dma")
        ex_done = sem("ex_done")
        ex_act = sem("ex_act")
        masked = sem("masked")
        pv_done = sem("pv_done")
        oT_ev = sem("oT_ev")
        o_done = sem("o_done")
        rden_s = sem("rden_s")
        attn_s = sem("attn_s")
        aT_done = sem("aT_done")
        aT_hs = sem("aT_hs")
        aT_ls = sem("aT_ls")
        wo_done = sem("wo_done")
        res = sem("res")
        stat = sem("stat")
        mv = sem("mv")
        rs = sem("rs")
        ln = sem("ln")
        x1_out = shared.x1_out
        spare_pool, spare_dve = sem("spare_pool"), sem("spare_dve")
        PER_T, PER_SPILL, PER_STACK, PER_NM = 4, 4 * 16, 8 * 16, 2 * 16

        block = ctx.enter_context(nc.Block())

        @block.sync
        def _(sp):
            sp.dma_start(xT_sb[:], xT[0].rearrange("(c p) n -> p c n", p=P)).then_inc(xT_in, 16)
            sp.dma_start(prob[0][0][:, 0:NC, :].rearrange("p a b -> p (a b)")[:, 0:2 * S],
                         wqkvT.rearrange("(c p) n -> p c n", p=P)[:, :, 0:S]).then_inc(w_in, 16)
            sp.dma_start(prob[0][1][:, 0, :].rearrange("p (c n) -> p c n", c=NC),
                         wqkvT.rearrange("(c p) n -> p c n", p=P)[:, :, S:]).then_inc(w_in, 16)
            sp.dma_start(prob[0][1][:, 1, :].rearrange("p (c n) -> p c n", c=NC),
                         woT.rearrange("(c p) n -> p c n", p=P)).then_inc(w_in, 16)
            for dst, src in ((cos_sb, cos), (sin_sb, sin)):
                sp.dma_start(dst[:], src.rearrange("(t p) a d -> p t a d", p=P)).then_inc(w_in, 16)

            def load_xT(b):
                sp.wait_ge(x_split, 2 * b)
                sp.dma_start(xT_sb[:], xT[b].rearrange("(c p) n -> p c n", p=P)).then_inc(xT_in, 16)

            def spill_parts(b, n, par):
                dst = (q_parts, k_parts)[n // 2][par, 8 * (n % 2):8 * (n % 2) + 8]
                for src, there, e in ((part_h, qkT_h, (1, 0)[n // 2]), (part_l, qkT_l, (0, 1)[n // 2])):
                    sp.wait_ge(there, PER_T * b + n + 1)
                    sp.dma_start(dst[:, DH * e:DH * e + DH], src[:, n % 2, :].bitcast(f32)).then_inc(spill[n % 2], 16)

            def fill_stack(b, qk, par):
                for i in range(2):
                    sp.wait_ge(spill[i], PER_SPILL * b + 32 * (qk + 1))
                dst = (q_st, k_st)[qk][par]
                for hp in range(2):
                    src = (q_parts, k_parts)[qk][par].rearrange("(hh hp) r n -> hp r hh n", hp=2)[hp]
                    for to, at, n in (((0, 0, 2 * DH), (2 * DH, DH, DH + 2)),
                                      ((0, 0, DH), (DH, 0, 2 * DH)))[qk]:
                        lo = ROWS * hp + to
                        sp.dma_start(dst[lo:lo + n].bitcast(f32), src[at:at + n]).then_inc(stack, 16)

            def place_maxima(b, par):
                sp.wait_ge(nmT_ev, b + 1)
                sp.dma_start(maxima, nmaxT[:].bitcast(f32)).then_inc(nm_spill, 16)
                sp.wait_ge(nm_spill, 16 * (b + 1))
                for hp in range(2):
                    at = ROWS * hp + ROWS_QK
                    sp.dma_start(q_st[par][at:at + 2].bitcast(f32),
                                 maxima.rearrange("(hp hh e) n -> hp e hh n", hp=2, e=2)[hp]
                                 ).then_inc(nm_dma, 16)

            def load_x(b):
                sp.dma_start(y_sb[:], x[b].rearrange("(t p) d -> p t d", p=P)).then_inc(x_in, 16)

            def store_x1(b):
                sp.wait_ge(ln, NT * (b + 1))
                sp.dma_start(x1[b].rearrange("(t p) d -> p t d", p=P), y_sb[:]).then_inc(x1_out, 16)
                if not (isinstance(b, int) and b == B - 1):
                    sp.wait_ge(x1_out, 16 * (b + 1))

            def load_ffn_weights():
                sp.wait_ge(pv_done, NT * NG * (B - 1))
                for dst, src in zip(shared.raw_weights(), ffn_weights):
                    sp.dma_start(dst, src).then_inc(shared.weights_in, 16)
                sp.dma_start(shared.xr(), x1[0].rearrange("(t p) d -> p t d", p=P)).then_inc(shared.xr_in, 16)

            def iteration(b, par, E=True, M=True, F=True, X=True):
                if F:
                    for n in range(4):
                        spill_parts(b + 2, n, par)
                    if E:
                        sp.wait_ge(ex_done, STEPS * (b + 1))
                    fill_stack(b + 2, 0, par)
                if M:
                    place_maxima(b + 1, 1 - par)
                if F:
                    fill_stack(b + 2, 1, par)
                if X:
                    load_xT(b + 4)
                if isinstance(b, int) and b == B - 1:
                    load_ffn_weights()
                if E:
                    store_x1(b)
                if M:
                    load_x(b + 1)

            sp.wait_ge(set_s, 1)
            for par in range(2):
                sp.dma_start(q_parts[par, :, 2 * DH:].rearrange("h e n -> e h n"),
                             zeros[0:2, None, :].broadcast_to([2, H, S])).then_inc(pad_in, 16)
                for st, row in ((q_st, zeros), (k_st, ones)):
                    for hp in range(2):
                        lo = ROWS * hp + ROWS_QK
                        sp.dma_start(st[par][lo:lo + DH].bitcast(f32),
                                     row[:, None, :].broadcast_to([DH, HH, S])).then_inc(pad_in, 16)
            load_xT(1)
            sp.wait_ge(pad_in, 10 * 16)
            iteration(-2, 0, E=False, M=False)
            iteration(-1, 1, E=False)
            with sp.Fori(0, 2) as i:
                iteration(2 * i, 0)
                iteration(2 * i + 1, 1)
            iteration(4, 0, X=False)
            iteration(5, 1, X=False)
            iteration(6, 0, F=False, X=False)
            iteration(7, 1, M=False, F=False, X=False)

        def rope_op(engine, nc_engine, b, n):
            t, k = n // 3, n % 3
            raw = qk_raw[:, t % 2, :].rearrange("p (a h d) -> p a h d", a=2, h=H)
            rot = qk_rot[:, t, :]
            first = isinstance(b, int) and b == 0
            if k == 0:
                engine.wait_ge(qk_ev, NT * b + t + 1)
                if not first:
                    engine.wait_ge(qkT_done, PER_T * b)
                nc_engine.tensor_tensor(rot.rearrange("p (a h d) -> p a h d", a=2, h=H), raw,
                                        cos_sb[:, t, :, None, :].broadcast_to([P, 2, H, DH]),
                                        ALU.mult).then_inc(rope, 1)
            elif k == 1:
                if not (first and t == 0):
                    engine.wait_ge(rope, 3 * NT * b + n - 1)
                nc_engine.tensor_tensor(rope_s[:].rearrange("p (a h d) -> p a h d", a=2, h=H), raw,
                                        sin_sb[:, t, :, None, :].broadcast_to([P, 2, H, DH]),
                                        ALU.mult).then_inc(rope, 1)
            else:
                engine.wait_ge(rope, 3 * NT * b + n)
                nc_engine.tensor_tensor(rot.rearrange("p (n e) -> p n e", e=2),
                                        rot.rearrange("p (n e) -> p n e", e=2),
                                        rope_s[:].rearrange("p (n e) -> p n e", e=2)[:, :, ::-1],
                                        ALU.add).then_inc(rope, 1)

        def small_bank(b, n):
            if isinstance(b, int) and b == 0:
                return (mi_ps, mx_ps[0], mx_ps[1], pv_ps)[n][:]
            return mi_ps[:]

        def max_bank(b, f):
            if isinstance(b, int) and b == 0:
                return (mx_ps[0][:], mx_ps[1][:], ex_ps[0][:, 0, :], ex_ps[0][:, 1, :])[f % 4]
            return mx_ps[f % 2][:]

        @block.gpsimd
        def _(pool):
            nc.gpsimd.memset(ident[:], 0.0).then_inc(const_s, 1)
            nc.gpsimd.memset(mask_b[:], 0.0).then_inc(const_s, 1)
            nc.gpsimd.memset(mhalf[:], -0.5).then_inc(const_s, 1)
            pool.wait_ge(const_s, 3)
            nc.gpsimd.affine_select(out=ident[:], in_=ident[:], compare_op=ALU.not_equal, fill=1.0, base=0,
                                    pattern=[[-1, P]], channel_multiplier=1).then_inc(const_s, 1)
            nc.gpsimd.affine_select(out=mask_b[:], in_=mask_b[:], compare_op=ALU.is_ge, fill=NEG, base=0,
                                    pattern=[[0, 2], [-1, P]], channel_multiplier=1).then_inc(const_s, 1)
            pool.wait_ge(const_s, 5)
            nc.gpsimd.tensor_copy(ident_b[:], ident[:]).then_inc(idb_s, 1)

            def split_x(b, par):
                if not (isinstance(b, int) and b < 2):
                    pool.wait_ge(v_done, NT * (b - 1))
                wait_apart(pool, spare_pool, xT_in, 16 * (b + 1))
                nc.gpsimd.tensor_scalar(xh[par][:], xT_sb[:], 1.0, None, ALU.mult).then_inc(x_split, 1)
                pool.wait_ge(x_split, 2 * b + 1)
                nc.gpsimd.tensor_tensor(xl[par][:], xT_sb[:], xh[par][:].bitcast(f32),
                                        ALU.subtract).then_inc(x_split, 1)

            def mask(b, m):
                j, kt = m // NT, m % NT
                p = prob[kt][j % 2 if kt < 2 else 0]
                wait_apart(pool, spare_pool, ex_act, STEPS * b + 2 * m + 2)
                nc.gpsimd.affine_select(out=p[:, :, 0:P], in_=p[:, :, 0:P], compare_op=ALU.is_ge, fill=0.0,
                                        base=0, pattern=[[0, G4], [1, P]],
                                        channel_multiplier=-1).then_inc(masked, 1)

            def iteration(b, par, E=True, M=True, F=True, X=True):
                for m in range(4 * NG):
                    if E:
                        mask(b, m)
                    if F and ROPE_MASK * m < 3 * NT and not (isinstance(b, int) and b == -2):
                        for n in range(ROPE_MASK):
                            rope_op(pool, nc.gpsimd, b + 2, ROPE_MASK * m + n)
                    if X and m == X_AFTER:
                        split_x(b + 3, 1 - par)
                if E:
                    wait_apart(pool, spare_pool, mv, NT * (b + 1))
                    nc.gpsimd.tensor_scalar(vare[:], meanvar[:, :, 1], EPS, None, ALU.add).then_inc(rs, 1)
                    pool.wait_ge(rs, 2 * b + 1)
                    nc.gpsimd.tensor_tensor(rstd[:], vare[:], mhalf[:], ALU.pow).then_inc(rs, 1)

            split_x(0, 0)
            iteration(-2, 0, E=False, M=False)
            iteration(-1, 1, E=False)
            with pool.Fori(0, 2) as i:
                iteration(2 * i, 0)
                iteration(2 * i + 1, 1)
            iteration(4, 0)
            iteration(5, 1, X=False)
            iteration(6, 0, F=False, X=False)
            iteration(7, 1, M=False, F=False, X=False)

        @block.scalar
        def _(act):
            act.wait_ge(w_in, 5 * 16)
            raw_qk = prob[0][0][:, 0:NC, :]
            raw_v = prob[0][1][:, 0, :].rearrange("p (c n) -> p c n", c=NC)
            raw_o = prob[0][1][:, 1, :].rearrange("p (c n) -> p c n", c=NC)
            nc.scalar.activation(wqkv_h[:, :, 0:S], raw_qk, ACT.Copy).then_inc(w_split, 1)
            nc.scalar.activation(wqkv_h[:, :, S:], raw_v, ACT.Copy).then_inc(w_split, 1)
            nc.scalar.activation(wo_h[:], raw_o, ACT.Copy).then_inc(w_split, 1)

            def ev_qk(b, t):
                act.wait_ge(qk_done, NT * b + t + 1)
                if not (isinstance(b, int) and NT * b + t < 2):
                    act.wait_ge(rope, 3 * (NT * b + t - 1) - 1)
                nc.scalar.activation(qk_raw[:, t % 2, :], small_bank(b, t), ACT.Copy).then_inc(qk_ev, 1)

            def ev_v(b, t, par):
                act.wait_ge(v_done, NT * b + t + 1)
                nc.scalar.activation(v_sb[par][:, t, :, 0:DH],
                                     ex_ps[1][:, t % 2, 0:D].rearrange("p (h d) -> p h d", h=H),
                                     ACT.Copy).then_inc(v_ev, 1)

            def high_qkT(b, n):
                act.wait_ge(qkT_done, PER_T * b + n + 1)
                if n >= 2:
                    act.wait_ge(spill[n % 2], PER_SPILL * b + 32)
                nc.scalar.activation(part_h[:, n % 2, :], small_bank(b, n), ACT.Copy).then_inc(qkT_h, 1)

            def exp_step(b, s):
                j, kt, pr = s // 8, s % 8 // 2, s % 2
                p = prob[kt][j % 2 if kt < 2 else 0]
                act.wait_ge(ex_done, STEPS * b + s + 1)
                if kt < 2 and j >= 2:
                    act.wait_ge(pv_done, NT * (NG * b + j - 2) + kt + 1)
                if kt >= 2 and j >= 1:
                    act.wait_ge(pv_done, NT * (NG * b + j - 1) + kt + 1)
                n = S - P * kt
                nc.scalar.activation(p[:, 2 * pr:2 * pr + 2, :], ex_ps[s % 2][:, :, 0:n],
                                     ACT.Exp).then_inc(ex_act, 1)

            def ev_oT(b, j):
                act.wait_ge(pv_done, NT * (NG * b + j + 1))
                nc.scalar.activation(oT_sb[:, j, :], pv_ps[:], ACT.Copy).then_inc(oT_ev, 1)

            def iteration(b, par, E=True, M=True, F=True):
                for s in range(STEPS):
                    if E:
                        exp_step(b, s)
                    if F and s in QK_AT:
                        ev_qk(b + 2, QK_AT[s])
                    if F and s in T_AT:
                        high_qkT(b + 2, T_AT[s])
                    if E and s in OT_AT:
                        ev_oT(b, OT_AT[s])
                if E:
                    ev_oT(b, NG - 1)
                if M:
                    act.wait_ge(nmT_done, b + 2)
                    if not (isinstance(b, int) and b < 0):
                        act.wait_ge(nm_spill, 16 * (b + 1))
                    nc.scalar.activation(nmaxT[:], ex_ps[0][0:2 * H, 0, :], ACT.Copy).then_inc(nmT_ev, 1)
                if F:
                    for t in range(2):
                        ev_v(b + 2, t, par)
                if E:
                    for c in range(NC):
                        act.wait_ge(aT_done, NC * b + c + 1)
                        nc.scalar.activation(aT_h[:, c, :], mx_ps[c][:], ACT.Copy).then_inc(aT_hs, 1)
                if F:
                    for t in range(2, NT):
                        ev_v(b + 2, t, par)

            act.wait_ge(set_s, 4)
            iteration(-2, 0, E=False, M=False)
            iteration(-1, 1, E=False)
            with act.Fori(0, 3) as i:
                iteration(2 * i, 0)
                iteration(2 * i + 1, 1)
            iteration(6, 0, F=False)
            iteration(7, 1, M=False, F=False)

        @block.vector
        def _(dve):
            nc.vector.memset(zeros, 0.0)
            nc.vector.memset(ones, 1.0).then_inc(set_s, 1)
            for i in range(2):
                nc.vector.memset(v_sb[i][:], 1.0).then_inc(set_s, 1)
            nc.vector.memset(bmax[:], NEG).then_inc(set_s, 1)
            raw_qk = prob[0][0][:, 0:NC, :]
            raw_v = prob[0][1][:, 0, :].rearrange("p (c n) -> p c n", c=NC)
            raw_o = prob[0][1][:, 1, :].rearrange("p (c n) -> p c n", c=NC)
            dve.wait_ge(w_split, 3)
            nc.vector.tensor_tensor(wqkv_l[:, :, 0:S], raw_qk, wqkv_h[:, :, 0:S].bitcast(f32),
                                    ALU.subtract).then_inc(w_split, 1)
            nc.vector.tensor_tensor(wqkv_l[:, :, S:], raw_v, wqkv_h[:, :, S:].bitcast(f32),
                                    ALU.subtract).then_inc(w_split, 1)
            nc.vector.tensor_tensor(wo_l[:], raw_o, wo_h[:].bitcast(f32), ALU.subtract).then_inc(w_split, 1)

            def low_qkT(b, n):
                dve.wait_ge(qkT_h, PER_T * b + n + 1)
                nc.vector.tensor_tensor(part_l[:, n % 2, :], small_bank(b, n), part_h[:, n % 2, :].bitcast(f32),
                                        ALU.subtract).then_inc(qkT_l, 1)

            def block_max(b, f):
                pair, hp, kind = FILL_KIND[f % len(FILL_KIND)]
                head = 2 * (f // len(FILL_KIND) * 2 + pair) + hp
                heads = slice(head, head + 3, 2) if kind == Q1 else slice(head, head + 1)
                n = {Q3: 1, Q02: 4, Q1: 2}[kind]
                dve.wait_ge(mx_done, FILLS * b + f + 1)
                nh = 2 if kind == Q1 else 1
                nc.vector.tensor_reduce(out=bmax[:, heads, SLOT[kind]:SLOT[kind] + n],
                                        in_=max_bank(b, f).rearrange("p (h n k) -> p h n k", h=nh, n=n),
                                        axis=AX.X, op=ALU.max).then_inc(mx_read, 1)

            def negate_max(b):
                dve.wait_ge(mx_read, FILLS * (b + 1))
                nc.vector.tensor_reduce(out=nmax[:], in_=bmax[:].rearrange("p h (w s) -> p h w s", w=NT),
                                        axis=AX.X, op=ALU.max, negate=True).then_inc(nm, 1)
                dve.wait_ge(nm, 4 * b + 1)
                nc.vector.tensor_copy(nmax_h[:], nmax[:]).then_inc(nm, 1)
                dve.wait_ge(nm, 4 * b + 2)
                view = nmax2[:].rearrange("p w (hp hh e) -> p e hp hh w", hp=2, e=2)
                src = [a.rearrange("p (hh hp) w -> p hp hh w", hp=2) for a in (nmax[:], nmax_h[:].bitcast(f32))]
                nc.vector.tensor_copy(view[:, 0], src[1]).then_inc(nm, 1)
                nc.vector.tensor_tensor(view[:, 1], src[0], src[1], ALU.subtract).then_inc(nm, 1)

            def normalise(b, t):
                o = (mx_ps[0], mx_ps[1], mi_ps, pv_ps)[t][:].rearrange("p (h c) -> p h c", h=H)
                dve.wait_ge(o_done, NT * b + t + 1)
                nc.vector.reciprocal(rden[:, t], o[:, :, DH:DH + 1]).then_inc(rden_s, 1)
                dve.wait_ge(rden_s, NT * b + t + 1)
                nc.vector.tensor_tensor(attn[:, t, :].rearrange("p (h d) -> p h d", h=H), o[:, :, 0:DH],
                                        rden[:, t].broadcast_to([P, H, DH]), ALU.mult).then_inc(attn_s, 1)

            def low_aT(b, c):
                dve.wait_ge(aT_hs, NC * b + c + 1)
                nc.vector.tensor_tensor(aT_l[:, c, :], mx_ps[c][:], aT_h[:, c, :].bitcast(f32),
                                        ALU.subtract).then_inc(aT_ls, 1)

            def residual(b, u):
                dve.wait_ge(wo_done, 2 * b + u + 1)
                if u == 0:
                    dve.wait_ge(x_in, 16 * (b + 1))
                y = y_sb[:, 2 * u:2 * u + 2, :]
                nc.vector.tensor_tensor(y, (mi_ps, pv_ps)[u][:].rearrange("p (t d) -> p t d", t=2), y,
                                        ALU.add).then_inc(res, 1)

            def iteration(b, par, E=True, M=True, F=True):
                if isinstance(b, int) and b == -2:
                    for n in range(3 * NT):
                        rope_op(dve, nc.vector, 0, n)
                for s in range(STEPS):
                    if M and s in FILL_STEP:
                        for f in FILL_STEP[s]:
                            block_max(b + 1, f)
                    if F and s in T_AT:
                        low_qkT(b + 2, T_AT[s])
                if M:
                    negate_max(b + 1)
                if isinstance(b, int) and b == B - 1:
                    split_ffn_weights()
                if E:
                    for t in range(NT):
                        normalise(b, t)
                    for c in range(NC):
                        low_aT(b, c)
                    for u in range(2):
                        residual(b, u)
                    for t in range(NT):
                        dve.wait_ge(res, 2 * (b + 1) + t // 2 + 1)
                        nc.vector.bn_stats(stats[:, t, :], y_sb[:, t, :]).then_inc(stat, 1)
                    for t in range(NT):
                        wait_apart(dve, spare_dve, stat, NT * b + t + 1)
                        nc.vector.bn_aggr(meanvar[:, t, :], stats[:, t, :]).then_inc(mv, 1)
                if E:
                    dve.wait_ge(rs, 2 * (b + 1))
                    for t in range(NT):
                        nc.vector.tensor_scalar(y_sb[:, t, :], y_sb[:, t, :], meanvar[:, t, 0:1],
                                                rstd[:, t:t + 1], ALU.subtract, ALU.mult).then_inc(ln, 1)

            def split_ffn_weights():
                views = []
                for pair, raw in zip((shared.gate, shared.up), shared.raw_weights()):
                    v = raw.rearrange("p c (a q j) -> p c a j q", a=HALVES, j=4)
                    for c in range(NC):
                        for a in range(HALVES):
                            views.append([pair[:, part, c, 4 * a:4 * a + 4, :] for part in range(2)] + [v[:, c, a]])
                dve.wait_ge(shared.weights_in, 4 * 16)
                for high, _, raw in views:
                    nc.vector.tensor_copy(high, raw).then_inc(shared.w_parts, 1)
                for n, (high, low, raw) in enumerate(views):
                    dve.wait_ge(shared.w_parts, n + 1)
                    nc.vector.tensor_tensor(low, raw, high.bitcast(f32), ALU.subtract).then_inc(shared.w_parts, 1)

            dve.sem_inc(res, 2)
            dve.wait_ge(w_in, 5 * 16)
            iteration(-2, 0, E=False, M=False)
            iteration(-1, 1, E=False)
            with dve.Fori(0, 3) as i:
                iteration(2 * i, 0)
                iteration(2 * i + 1, 1)
            iteration(6, 0, F=False)
            iteration(7, 1, M=False, F=False)

        @block.tensor
        def _(pe):
            def product(out, lh, ll, rh, rl, chunks, inc):
                terms = [(a, r, c) for c in range(chunks) for a, r in ((lh, rh), (lh, rl), (ll, rh))]
                for n, (a, r, c) in enumerate(terms):
                    last = nc.tensor.matmul(out, a(c), r(c), start=n == 0, stop=n == len(terms) - 1)
                last.then_inc(inc, 1)

            def project_qk(b, t, par):
                tok = slice(P * t, P * t + P)
                product(small_bank(b, t), lambda c: xh[par][:, c, tok], lambda c: xl[par][:, c, tok],
                        lambda c: wqkv_h[:, c, 0:2 * D], lambda c: wqkv_l[:, c, 0:2 * D], NC, qk_done)

            def project_v(b, t, par):
                tok = slice(P * t, P * t + P)
                product(ex_ps[1][:, t % 2, 0:D], lambda c: xh[par][:, c, tok], lambda c: xl[par][:, c, tok],
                        lambda c: wqkv_h[:, c, 2 * D:], lambda c: wqkv_l[:, c, 2 * D:], NC, v_done)

            def transpose_qk(b, n):
                for t in range(NT):
                    last = nc.tensor.transpose(small_bank(b, n)[:, P * t:P * t + P], qk_rot[:, t, P * n:P * n + P], ident[:])
                last.then_inc(qkT_done, 1)

            def max_block(b, f, par):
                pair, hp, kind = FILL_KIND[f % len(FILL_KIND)]
                hh = f // len(FILL_KIND) * 2 + pair
                rows = slice(ROWS * hp, ROWS * hp + ROWS)
                banks = 4 if isinstance(b, int) and b == 0 else 2
                if f >= banks:
                    pe.wait_ge(mx_read, FILLS * b + f - banks + 1)
                if f == 0:
                    pe.wait_ge(stack, PER_STACK * (b + 1))
                out = max_bank(b, f)

                def scores(at, hh, qt):
                    return nc.tensor.matmul(out[:, at:at + (qt + 1) * P], q_st[par][rows, hh, P * qt:P * qt + P],
                                            k_st[par][rows, hh, 0:(qt + 1) * P], start=False, stop=True,
                                            skip_group_check=True)

                first, step = {Q3: (3, 1), Q02: (0, 3), Q1: (1, 2)}[kind]
                diagonals = out.rearrange("p (n k) -> p n k", n=NT)[:, first:NT:step, :]
                nc.tensor.matmul(diagonals, ident_b[:], mask_b[:, 0:1 if kind == Q3 else 2, :], start=True,
                                 stop=False, skip_group_check=True)
                if kind == Q3:
                    last = scores(0, hh, 3)
                elif kind == Q02:
                    scores(0, hh, 0)
                    last = scores(P, hh, 2)
                else:
                    scores(0, hh, 1)
                    last = scores(2 * P, hh + 1, 1)
                last.then_inc(mx_done, 1)

            def score_step(b, s, par, M):
                j, kt, pr = s // 8, s % 8 // 2, s % 2
                if s == 0:
                    pe.wait_ge(nm_dma, PER_NM * (b + 1))
                if s >= 2:
                    pe.wait_ge(ex_act, STEPS * b + s - 1)
                if s == 1 and M:
                    pe.wait_ge(v_ev, NT * (b + 2))
                hh = 2 * j + pr
                for hp in range(2):
                    rows = slice(ROWS * hp, ROWS * hp + ROWS)
                    last = nc.tensor.matmul(ex_ps[s % 2][:, hp, 0:S - P * kt], k_st[par][rows, hh, P * kt:P * kt + P],
                                            q_st[par][rows, hh, P * kt:], start=True, stop=True)
                last.then_inc(ex_done, 1)

            def pv(b, j, kt, par):
                if kt == 0:
                    if j == 0:
                        pe.wait_ge(v_ev, NT * (b + 1))
                        pe.wait_ge(res, 2 * (b + 1))
                    else:
                        pe.wait_ge(oT_ev, NG * b + j)
                pe.wait_ge(masked, 4 * NG * b + NT * j + kt + 1)
                for g in range(G4):
                    last = nc.tensor.matmul(pv_ps[32 * g:32 * g + 32, P * kt:],
                                            v_sb[par][:, kt, G4 * j + g, :],
                                            prob[kt][j % 2 if kt < 2 else 0][:, g, :],
                                            start=kt == 0, stop=kt == NT - 1, skip_group_check=True)
                last.then_inc(pv_done, 1)

            def output_heads(b):
                pe.wait_ge(oT_ev, NG * (b + 1))
                for k in range(NT):
                    for j in range(NG):
                        last = nc.tensor.transpose((mx_ps[0], mx_ps[1], mi_ps, pv_ps)[k][:, P * j:P * j + P],
                                                   oT_sb[:, j, P * k:P * k + P], ident[:])
                    last.then_inc(o_done, 1)

            def output_transposes(b):
                pe.wait_ge(attn_s, NT * (b + 1))
                for c in range(NC):
                    for t in range(NT):
                        last = nc.tensor.transpose(mx_ps[c][:, P * t:P * t + P], attn[:, t, P * c:P * c + P], ident[:])
                    last.then_inc(aT_done, 1)

            def output_product(b):
                pe.wait_ge(aT_ls, NC * (b + 1))
                for u in range(2):
                    for v in range(2):
                        tok = slice(P * (2 * u + v), P * (2 * u + v) + P)
                        terms = [(a, r, c) for c in range(NC) for a, r in ((aT_h, wo_h), (aT_h, wo_l), (aT_l, wo_h))]
                        for n, (a, r, c) in enumerate(terms):
                            last = nc.tensor.matmul((mi_ps, pv_ps)[u][:, D * v:D * v + D], a[:, c, tok], r[:, c, :],
                                                    start=n == 0, stop=n == len(terms) - 1)
                    last.then_inc(wo_done, 1)

            def v_tiles(b, tiles, par, E):
                for t in tiles:
                    if t >= 2:
                        pe.wait_ge(v_ev, NT * b + t - 1)
                    elif E:
                        pe.wait_ge(ex_act, STEPS * (b - 1))
                    project_v(b, t, par)

            def stay_warm(b, s, n):
                if s == 2:
                    pe.wait_ge(res, 2 * (b + 1))
                for _ in range(n):
                    nc.tensor.matmul(mi_ps[:], wqkv_h[:, 0, 0:P], wqkv_h[:, 0, 0:S], start=True, stop=True)

            def stack_transposes(b, n):
                if n == 0:
                    pe.wait_ge(rope, 3 * NT * (b + 1))
                elif not (isinstance(b, int) and b == 0):
                    pe.wait_ge(qkT_l, PER_T * b + n)
                transpose_qk(b, n)

            def transpose_maxima(b, E):
                if E:
                    pe.wait_ge(ex_act, STEPS * b - 1)
                pe.wait_ge(nm, 4 * (b + 1))
                for w, t in enumerate(WTILE):
                    last = nc.tensor.transpose(ex_ps[0][0:2 * H, 0, P * t:P * t + P], nmax2[:, w, :], ident[:])
                last.then_inc(nmT_done, 1)

            def iteration(b, par, E=True, M=True, F=True):
                for s in range(STEPS):
                    if E:
                        score_step(b, s, par, M)
                    fills = FILL_STEP.get(s, range(0)) if M else range(0)
                    for f in fills[:1]:
                        max_block(b + 1, f, 1 - par)
                    if F and s in QK_AT:
                        t = QK_AT[s]
                        if t == 0:
                            pe.wait_ge(x_split, 2 * (b + 3))
                            if E:
                                pe.wait_ge(res, 2 * (b + 1))
                            elif M:
                                pe.wait_ge(qkT_l, PER_T)
                        elif not (isinstance(b, int) and b == -2):
                            pe.wait_ge(qk_ev, NT * (b + 2) + t)
                        project_qk(b + 2, t, par)
                    if F and s in T_AT:
                        stack_transposes(b + 2, T_AT[s])
                    if E and s in PV_AT:
                        pv(b, *PV_AT[s], par)
                    for f in fills[1:]:
                        max_block(b + 1, f, 1 - par)
                    if not F and s >= 2:
                        stay_warm(b, s, WARM_6 if M else WARM_7)
                if E:
                    for kt in range(NT):
                        pv(b, NG - 1, kt, par)
                if M:
                    transpose_maxima(b + 1, E)
                if E:
                    if F:
                        pe.wait_ge(qkT_l, PER_T * (b + 3))
                    else:
                        pe.wait_ge(res, 2 * (b + 1))
                    output_heads(b)
                if F:
                    v_tiles(b + 2, range(2), par, E)
                if E:
                    output_transposes(b)
                if F:
                    v_tiles(b + 2, range(2, NT), par, E)
                if E:
                    output_product(b)
                if isinstance(b, int) and b == B - 1:
                    pe.wait_ge(ex_act, STEPS * B)
                    for _ in range(WARM_END):
                        nc.tensor.matmul(ex_ps[0][:, 0, :], wqkv_h[:, 0, 0:P], wqkv_h[:, 0, 0:S], start=True, stop=True)

            pe.wait_ge(idb_s, 1)
            pe.wait_ge(w_split, 6)
            iteration(-2, 0, E=False, M=False)
            iteration(-1, 1, E=False)
            with pe.Fori(0, 3) as i:
                iteration(2 * i, 0)
                iteration(2 * i + 1, 1)
            iteration(6, 0, F=False)
            iteration(7, 1, M=False, F=False)


NK = I // P
HALVES = NK // 4
CMP = 10
HIGHS = 2 * HALVES
LN_STEPS = 4
DOWN_AFTER = {5: (0,), 6: (1,), 7: (2, 3)}
XT_AFTER = {1: 0, 5: 1}


def ffn_phase(nc, x1, out, shared):
    ctx = ExitStack()
    with ctx:
        def sb(name, shape, dt=f32):
            return ctx.enter_context(nc.sbuf_tensor(name, shape, dt))

        def sem(name):
            return ctx.enter_context(nc.semaphore(name))

        def ps(name, shape):
            return ctx.enter_context(nc.psum_tensor(name, shape, f32))

        wg_h, wg_l, wu_h, wu_l = [pair[:, part] for pair in (shared.gate, shared.up) for part in range(2)]
        wd_h, wd_l = [sb(n, [P, NK, D], f32r) for n in ("wd_h", "wd_l")]
        ident = shared.ident
        mhalf = sb("mhalf2", [P, NT])
        xr = shared.xr()
        xh = [sb(f"x1h{i}", [P, NC, S], f32r) for i in range(2)]
        xl = [sb(f"x1l{i}", [P, NC, S], f32r) for i in range(2)]
        h = shared.halves()
        g_sb = shared.qk_raw
        y_sb = [shared.xT_sb[:].rearrange("p c (t d) -> p (c t) d", d=D), shared.y_sb[:]]
        mag = sb("mag", [P, 4, S])
        ext = sb("ext", [P, 4, S])
        win = sb("win", [P, 2, 2, S], bf16)
        lim = sb("lim", [P, 4, S], bf16)
        hm_h = [sb(f"hm_h{i}", [P, NK, S], f32r) for i in range(2)]
        hm_l = [sb(f"hm_l{i}", [P, NK, S], f32r) for i in range(2)]
        stats = sb("stats2", [P, NT, 6])
        vare = sb("vare2", [P, NT])
        meanvar = [sb(f"meanvar2_{i}", [P, NT, 2]) for i in range(2)]
        rstd = [sb(f"rstd2_{i}", [P, NT]) for i in range(2)]
        mrstd = [sb(f"mrstd{i}", [P, NT]) for i in range(2)]

        g_ps = [ps(f"g_ps{i}", [P, S]) for i in range(2)]
        u_ps = [ps(f"u_ps{i}", [P, S]) for i in range(2)]
        d_ps = [ps(f"d_ps{i}", [P, S]) for i in range(2)]
        x_ps = ps("x_ps", [P, S])

        w_high = sem("f_w_high")
        w_low = sem("f_w_low")
        const_s = sem("f_const")
        xr_in = shared.xr_in
        y_in = sem("y_in")
        xt_done = sem("xt_done")
        xt_h = sem("xt_h")
        xt_l = sem("xt_l")
        g_done = sem("g_done")
        u_done = sem("u_done")
        silu_s = sem("silu_s")
        h_s = sem("h_s")
        mag_s = sem("mag_s")
        cmp_s = sem("cmp_s")
        hm_hs = sem("hm_hs")
        hm_ls = [sem(f"hm_ls{a}") for a in range(HALVES)]
        d_done = sem("d_done")
        res = sem("f_res")
        stat = sem("f_stat")
        mv = sem("f_mv")
        rs = sem("f_rs")
        ln = sem("f_ln")
        y_out = sem("y_out")
        spare_pool, spare_dve, spare_sp = sem("f_spare_pool"), sem("f_spare_dve"), sem("f_spare_sp")

        def down_bank(b, t):
            if isinstance(b, int) and b == B - 1:
                return (d_ps[0], d_ps[1], g_ps[0], g_ps[1])[t][:]
            return d_ps[t % 2][:]

        def x_bank(b, c):
            return (d_ps[0] if isinstance(b, int) and b == 0 and c == 1 else x_ps)[:]

        block = ctx.enter_context(nc.Block())

        @block.sync
        def _(sp):
            def load_xr(b):
                sp.wait_ge(xt_done, NC * b)
                sp.dma_start(xr, x1[b].rearrange("(t p) d -> p t d", p=P)).then_inc(xr_in, 16)

            def load_y(b, par):
                sp.dma_start(y_sb[par], x1[b].rearrange("(t p) d -> p t d", p=P)).then_inc(y_in, 16)

            def iteration(b, par, X=True, Dn=True):
                if Dn and not (isinstance(b, int) and b == B - 1):
                    sp.wait_ge(y_in, 16 * (b + 1))
                    load_y(b + 1, 1 - par)
                if X:
                    load_xr(b + 3)
                if Dn:
                    sp.wait_ge(ln, NT * (b + 1))
                    sp.dma_start(out[b].rearrange("(t p) d -> p t d", p=P), y_sb[par]).then_inc(y_out, 16)
                    wait_apart(sp, spare_sp, y_out, 16 * (b + 1))

            load_xr(1)
            sp.wait_ge(shared.x1_out, 16 * B)
            sp.wait_ge(w_low, 2)
            load_y(0, 0)
            iteration(-1, 1, Dn=False)
            with sp.Fori(0, 2) as i:
                iteration(2 * i, 0)
                iteration(2 * i + 1, 1)
            iteration(4, 0)
            for b in range(5, B):
                iteration(b, b % 2, X=False)

        @block.gpsimd
        def _(pool):
            nc.gpsimd.memset(mhalf[:], -0.5).then_inc(const_s, 1)
            pool.wait_ge(const_s, 1)

            def low_hm(b, par):
                pool.wait_ge(hm_hs, HIGHS * b + 2)
                nc.gpsimd.tensor_tensor(hm_l[par][:, 0:4, :], h[0][:], hm_h[par][:, 0:4, :].bitcast(f32),
                                        ALU.subtract).then_inc(hm_ls[0], 1)

            def layer_norm(b, par):
                wait_apart(pool, spare_pool, mv, NT * (b + 1))
                nc.gpsimd.tensor_scalar(vare[:], meanvar[par][:, :, 1], EPS, None, ALU.add).then_inc(rs, 1)
                pool.wait_ge(rs, LN_STEPS * b + 1)
                nc.gpsimd.tensor_tensor(rstd[par][:], vare[:], mhalf[:], ALU.pow).then_inc(rs, 1)
                pool.wait_ge(rs, LN_STEPS * b + 2)
                nc.gpsimd.tensor_tensor(mrstd[par][:], meanvar[par][:, :, 0], rstd[par][:], ALU.mult).then_inc(rs, 1)
                wait_apart(pool, spare_pool, rs, LN_STEPS * b + 3)
                nc.gpsimd.tensor_scalar(mrstd[par][:], mrstd[par][:], -1.0, None, ALU.mult).then_inc(rs, 1)

            low_hm(0, 0)
            with pool.Fori(0, 3) as i:
                low_hm(2 * i + 1, 1)
                layer_norm(2 * i, 0)
                low_hm(2 * i + 2, 0)
                layer_norm(2 * i + 1, 1)
            low_hm(7, 1)
            layer_norm(6, 0)
            layer_norm(7, 1)

        @block.scalar
        def _(act):
            raw = shared.raw_weights()

            def high_down(a):
                nc.scalar.activation(wd_h[:, 4 * a:4 * a + 4, :].rearrange("p k d -> p (k d)"), raw[2 + a],
                                     ACT.Copy).then_inc(w_high, 1)

            def high_x(b, c, par):
                act.wait_ge(xt_done, NC * b + c + 1)
                nc.scalar.activation(xh[par][:, c, :], x_bank(b, c), ACT.Copy).then_inc(xt_h, 1)

            def silu(b, k):
                act.wait_ge(g_done, NK * b + k + 1)
                if not (isinstance(b, int) and b == 0 and k < 2):
                    act.wait_ge(h_s, NK * b + k - 1)
                nc.scalar.activation(g_sb[:, k % 2, :], g_ps[k % 2][:], ACT.Silu).then_inc(silu_s, 1)

            def magnitude(b, a):
                act.wait_ge(h_s, NK * b + 4 * a + 4)
                if not (isinstance(b, int) and b == 0 and a == 0):
                    act.wait_ge(cmp_s, CMP * (HALVES * b + a - 1) + 3)
                nc.scalar.activation(mag[:], h[a][:], ACT.Abs).then_inc(mag_s, 1)

            def high_hm(b, a, par):
                for r in range(2):
                    act.wait_ge(cmp_s, CMP * (HALVES * b + a) + 9 + r)
                    nc.scalar.activation(hm_h[par][:, 4 * a + 2 * r:4 * a + 2 * r + 2, :], h[a][:, 2 * r:2 * r + 2, :],
                                         ACT.Copy).then_inc(hm_hs, 1)

            def apply_norm(b, par):
                act.wait_ge(rs, LN_STEPS * (b + 1))
                for t in range(NT):
                    nc.scalar.activation(y_sb[par][:, t, :], y_sb[par][:, t, :], ACT.Identity, bias=mrstd[par][:, t:t + 1],
                                         scale=rstd[par][:, t:t + 1]).then_inc(ln, 1)

            def iteration(b, par, G=True, X=True, Dn=True, norm=True):
                if G:
                    for k in range(NK):
                        silu(b + 1, k)
                        if norm and k == 2:
                            apply_norm(b - 1, 1 - par)
                        if X and k in XT_AFTER:
                            high_x(b + 2, XT_AFTER[k], par)
                        if k == 3 and Dn:
                            high_hm(b, 1, par)
                        if k == 4:
                            magnitude(b + 1, 0)
                        if k == 7:
                            high_hm(b + 1, 0, 1 - par)
                            magnitude(b + 1, 1)
                else:
                    high_hm(b, 1, par)
                    apply_norm(b - 1, 1 - par)

            for c in range(NC):
                high_x(0, c, 0)
            for a in range(HALVES):
                high_down(a)
            act.wait_ge(w_low, 2)
            iteration(-1, 1, Dn=False, norm=False)
            iteration(0, 0, norm=False)
            with act.Fori(0, 2) as i:
                iteration(2 * i + 1, 1)
                iteration(2 * i + 2, 0)
            iteration(5, 1)
            iteration(6, 0, X=False)
            iteration(7, 1, G=False, X=False)
            apply_norm(7, 1)

        @block.vector
        def _(dve):
            raw = shared.raw_weights()

            def low_down(a):
                dve.wait_ge(w_high, 1 + a)
                nc.vector.tensor_tensor(wd_l[:, 4 * a:4 * a + 4, :].rearrange("p k d -> p (k d)"), raw[2 + a],
                                        wd_h[:, 4 * a:4 * a + 4, :].rearrange("p k d -> p (k d)").bitcast(f32),
                                        ALU.subtract).then_inc(w_low, 1)

            def low_x(b, c, par):
                dve.wait_ge(xt_h, NC * b + c + 1)
                nc.vector.tensor_tensor(xl[par][:, c, :], x_bank(b, c), xh[par][:, c, :].bitcast(f32),
                                        ALU.subtract).then_inc(xt_l, 1)

            def product(b, k):
                dve.wait_ge(silu_s, NK * b + k + 1)
                dve.wait_ge(u_done, NK * b + k + 1)
                if k % 4 == 0 and not (isinstance(b, int) and b == 0):
                    dve.wait_ge(hm_ls[k // 4], (1 + k // 4) * b)
                nc.vector.tensor_tensor(h[k // 4][:, k % 4, :], u_ps[k % 2][:], g_sb[:, k % 2, :],
                                        ALU.mult).then_inc(h_s, 1)

            def compare(b, a, q):
                base = CMP * (HALVES * b + a)
                m = mag[:].rearrange("p (r e) n -> p r e n", r=2)
                if q == 0:
                    dve.wait_ge(mag_s, HALVES * b + a + 1)
                    if not (isinstance(b, int) and b == 0 and a == 0):
                        dve.wait_ge(cmp_s, base)
                    nc.vector.tensor_tensor(ext[:, 1:3, :], m[:, :, 0], m[:, :, 1], ALU.max).then_inc(cmp_s, 1)
                    nc.vector.tensor_tensor(ext[:, 0:4:3, :], m[:, :, 0], m[:, :, 1], ALU.min).then_inc(cmp_s, 1)
                elif q == 1:
                    nc.vector.tensor_tensor(win[:, :, 0], m[:, :, 0], m[:, :, 1], ALU.is_ge).then_inc(cmp_s, 1)
                    dve.wait_ge(cmp_s, base + 3)
                    nc.vector.tensor_scalar(win[:, :, 1], win[:, :, 0], -1.0, 1.0, ALU.mult,
                                            ALU.add).then_inc(cmp_s, 1)
                    nc.vector.tensor_tensor(lim[:, 0:2, :], ext[:, 0:2, :], ext[:, 2:4, :],
                                            ALU.is_ge).then_inc(cmp_s, 1)
                    dve.wait_ge(cmp_s, base + 5)
                    nc.vector.tensor_scalar(lim[:, 2:4, :], lim[:, 0:2, :], -1.0, 1.0, ALU.mult,
                                            ALU.add).then_inc(cmp_s, 1)
                elif q == 2:
                    dve.wait_ge(cmp_s, base + 6)
                    nc.vector.tensor_tensor(win[:], win[:], lim[:, 1:3, None, :].broadcast_to([P, 2, 2, S]),
                                            ALU.min).then_inc(cmp_s, 1)
                    dve.wait_ge(cmp_s, base + 7)
                    nc.vector.tensor_tensor(win[:], win[:], lim[:, 0:4:3, None, :].broadcast_to([P, 2, 2, S]),
                                            ALU.max).then_inc(cmp_s, 1)
                else:
                    dve.wait_ge(cmp_s, base + 8)
                    for r in range(2):
                        nc.vector.tensor_tensor(h[a][:, 2 * r:2 * r + 2, :], h[a][:, 2 * r:2 * r + 2, :],
                                                win[:, r], ALU.mult).then_inc(cmp_s, 1)

            def low_hm(b, par):
                for r in range(2):
                    k = 4 + 2 * r
                    dve.wait_ge(hm_hs, HIGHS * b + 3 + r)
                    nc.vector.tensor_tensor(hm_l[par][:, k:k + 2, :], h[1][:, 2 * r:2 * r + 2, :],
                                            hm_h[par][:, k:k + 2, :].bitcast(f32), ALU.subtract).then_inc(hm_ls[1], 1)

            def residual(b, t, par):
                dve.wait_ge(d_done, NT * b + t + 1)
                if t == 0:
                    dve.wait_ge(y_in, 16 * (b + 1))
                nc.vector.tensor_tensor(y_sb[par][:, t, :], down_bank(b, t)[:, 0:D], y_sb[par][:, t, :], ALU.add).then_inc(res, 1)

            def statistics(b, t, par):
                dve.wait_ge(res, NT * b + t + 1)
                nc.vector.bn_stats(stats[:, t, :], y_sb[par][:, t, :]).then_inc(stat, 1)

            def residual_and_statistics(b, t, par):
                residual(b, t, par)
                if t:
                    statistics(b, t - 1, par)
                if t == NT - 1:
                    statistics(b, t, par)
                    for n in range(NT):
                        wait_apart(dve, spare_dve, stat, NT * b + n + 1)
                        nc.vector.bn_aggr(meanvar[par][:, n, :], stats[:, n, :]).then_inc(mv, 1)

            def iteration(b, par, G=True, X=True, Dn=True):
                if G:
                    for k in range(NK):
                        if k == 4 and Dn:
                            low_hm(b, par)
                        product(b + 1, k)
                        if X and k in XT_AFTER:
                            low_x(b + 2, XT_AFTER[k], par)
                        if k < 3 and Dn:
                            compare(b, 1, k + 1)
                        if k >= 4:
                            compare(b + 1, 0, k - 4)
                        if Dn and k in DOWN_AFTER:
                            for t in DOWN_AFTER[k]:
                                residual_and_statistics(b, t, par)
                    compare(b + 1, 1, 0)
                else:
                    for q in range(1, 4):
                        compare(b, 1, q)
                    low_hm(b, par)
                    for t in range(NT):
                        residual_and_statistics(b, t, par)

            for c in range(NC):
                low_x(0, c, 0)
            for a in range(HALVES):
                low_down(a)
            iteration(-1, 1, Dn=False)
            with dve.Fori(0, 3) as i:
                iteration(2 * i, 0)
                iteration(2 * i + 1, 1)
            iteration(6, 0, X=False)
            iteration(7, 1, G=False, X=False)

        @block.tensor
        def _(pe):
            def project(b, k, par):
                first = isinstance(b, int) and b == 0 and k < 2
                if k == 0:
                    pe.wait_ge(xt_l, NC * (b + 1))
                for dst, wh, wl, read, inc in ((g_ps, wg_h, wg_l, silu_s, g_done), (u_ps, wu_h, wu_l, h_s, u_done)):
                    if not first:
                        pe.wait_ge(read, NK * b + k - 1)
                    n = 0
                    for c in range(NC):
                        for w, xx in ((wh, xh), (wh, xl), (wl, xh)):
                            last = nc.tensor.matmul(dst[k % 2][:], w[:, c, k, :], xx[par][:, c, :],
                                                    start=n == 0, stop=n == 3 * NC - 1)
                            n += 1
                    last.then_inc(inc, 1)

            def down_last(b, par):
                def terms(tiles, pairs, first=False, last=False):
                    for t in range(NT):
                        tok = slice(P * t, P * t + P)
                        todo = [(hm, w, k) for k in tiles for hm, w in pairs]
                        for n, (hm, w, k) in enumerate(todo):
                            product = nc.tensor.matmul(down_bank(b, t)[:, 0:D], hm[par][:, k, tok], w[:, k, :],
                                                       start=first and n == 0, stop=last and n == len(todo) - 1)
                        if last:
                            product.then_inc(d_done, 1)

                high = ((hm_h, wd_h), (hm_h, wd_l))
                low = ((hm_l, wd_h),)
                pe.wait_ge(res, NT * b)
                pe.wait_ge(hm_ls[0], b + 1)
                terms(range(4), high + low, first=True)
                for r in range(2):
                    pe.wait_ge(hm_hs, HIGHS * b + 3 + r)
                    terms(range(4 + 2 * r, 6 + 2 * r), high)
                pe.wait_ge(hm_ls[1], 2 * (b + 1))
                terms(range(4, NK), low, last=True)

            def down(b, t, par):
                if t == 0:
                    for a in range(HALVES):
                        pe.wait_ge(hm_ls[a], (1 + a) * (b + 1))
                if t >= 2:
                    pe.wait_ge(res, NT * b + t - 1)
                tok = slice(P * t, P * t + P)
                n = 0
                for k in range(NK):
                    for hm, w in ((hm_h, wd_h), (hm_h, wd_l), (hm_l, wd_h)):
                        last = nc.tensor.matmul(d_ps[t % 2][:, 0:D], hm[par][:, k, tok], w[:, k, :],
                                                start=n == 0, stop=n == 3 * NK - 1)
                        n += 1
                last.then_inc(d_done, 1)

            def transpose_x(b, c, first=False):
                if c == 0:
                    pe.wait_ge(xr_in, 16 * (b + 1))
                if not first:
                    pe.wait_ge(xt_l, NC * b + c)
                for t in range(NT):
                    last = nc.tensor.transpose(x_bank(b, c)[:, P * t:P * t + P], xr[:, t, P * c:P * c + P], ident[:])
                last.then_inc(xt_done, 1)

            def iteration(b, par, G=True, X=True, Dn=True):
                if G:
                    for k in range(NK):
                        project(b + 1, k, 1 - par)
                        if X and k in XT_AFTER:
                            transpose_x(b + 2, XT_AFTER[k])
                        if Dn and k in DOWN_AFTER:
                            for t in DOWN_AFTER[k]:
                                down(b, t, par)
                else:
                    down_last(b, par)

            for c in range(NC):
                transpose_x(0, c, first=True)
            iteration(-1, 1, Dn=False)
            pe.wait_ge(w_low, 2)
            with pe.Fori(0, 3) as i:
                iteration(2 * i, 0)
                iteration(2 * i + 1, 1)
            iteration(6, 0, X=False)
            iteration(7, 1, G=False, X=False)


def build(nc, x, xT, wqkvT, woT, wg, wu, wd, cos, sin, out):
    q_parts = nc.dram_tensor("q_parts", (2, H, ROWS_Q, S), f32, kind="Internal").ap()
    k_parts = nc.dram_tensor("k_parts", (2, H, 2 * DH, S), f32, kind="Internal").ap()
    maxima = nc.dram_tensor("maxima", (2 * H, S), f32, kind="Internal").ap()
    x1 = nc.dram_tensor("x1", (B, S, D), f32, kind="Internal").ap()
    gate, up = [w.rearrange("(c p) i -> p c i", p=P) for w in (wg, wu)]
    down = wd.rearrange("(a p j) d -> a p (j d)", a=HALVES, j=4)
    with ExitStack() as ctx:
        shared = Shared(nc, ctx)
        attention_phase(nc, x, xT, wqkvT, woT, cos, sin, [gate, up, *(down[a] for a in range(HALVES))],
                        q_parts, k_parts, maxima, x1, shared)
        ffn_phase(nc, x1, out, shared)


def kernel(**inputs):
    import numpy as np
    import concourse.bacc as bacc
    from concourse.bass_utils import run_bass_kernel_spmd as run

    a = {k: np.asarray(v) for k, v in inputs.items()}
    x = a["L0_attn_x"]
    inv = (1.0 / 10000.0 ** (np.arange(0, DH, 2, dtype=np.float32) / np.float32(DH))).astype(np.float32)
    ang = np.outer(np.arange(S, dtype=np.float32), inv).astype(np.float32)
    c2 = np.repeat(np.cos(ang), 2, axis=1)
    s2 = np.stack([np.sin(ang), -np.sin(ang)], axis=-1).reshape(S, DH)
    cos = np.stack([c2 / 4, c2], axis=1).astype(np.float32)
    sin = np.stack([s2 / 4, s2], axis=1).astype(np.float32)
    arrays = {
        "x": x,
        "xT": np.ascontiguousarray(x.transpose(0, 2, 1)),
        "wqkvT": np.ascontiguousarray(np.concatenate([a["L0_attn_W" + n].T for n in "qkv"], axis=1)),
        "woT": np.ascontiguousarray(a["L0_attn_Wo"].T),
        "w_gate": a["L0_ffn_w_gate"], "w_up": a["L0_ffn_w_up"], "w_down": a["L0_ffn_w_down"],
        "cos": cos, "sin": sin,
    }
    nc = bacc.Bacc("TRN2", target_bir_lowering=False, num_devices=1)
    args = [nc.dram_tensor(n, v.shape, mybir.dt.from_np(v.dtype), kind="ExternalInput").ap()
            for n, v in arrays.items()]
    out = nc.dram_tensor("out", (B, S, D), f32, kind="ExternalOutput").ap()
    build(nc, *args, out)
    r = run(nc, [arrays], core_ids=[0])
    return r.results[0]["out"]
```
